# Optimizing a Trainium2 kernel written in Bass

```python
import numpy as np
import jax
import jax.numpy as jnp

def _softmax(x, axis=-1):
    return jax.nn.softmax(x, axis=axis)

def _gelu(x):
    return jax.nn.gelu(x, approximate=True)

def _silu(x):
    return jax.nn.silu(x)

def _sigmoid(x):
    return jax.nn.sigmoid(x)

def _layernorm(x, axis=-1, eps=1e-05):
    m = jnp.mean(x, axis=axis, keepdims=True)
    v = jnp.var(x, axis=axis, keepdims=True)
    return (x - m) / jnp.sqrt(v + eps)

def _scatter_add(tgt, idx, src, axis=0):
    return tgt.at[idx].add(src)

def _segment_sum(src, seg, n):
    return jax.ops.segment_sum(src, seg, n)
kernel_name = 'mk_macaron_d1_jaxref_r2_87d737'

def setup_inputs(seed: int=0):
    np.random.seed(seed)
    _w = jnp.asarray

    def _L0_attn_setup():
        import jax, jax.numpy as jnp
        import numpy as np
        EPS = 1e-05
        NUM_HEADS = 16

        def _linear_attention(x, Wq, Wk, Wv, Wo, bo):
            B, L, E = x.shape
            H = NUM_HEADS
            D = E // H
            q = (x @ Wq.T).reshape(B, L, H, D)
            k = (x @ Wk.T).reshape(B, L, H, D)
            v = (x @ Wv.T).reshape(B, L, H, D)
            phi_q = jax.nn.elu(q) + 1.0
            phi_k = jax.nn.elu(k) + 1.0
            pq = jnp.moveaxis(phi_q, 1, 0)
            pk = jnp.moveaxis(phi_k, 1, 0)
            vt = jnp.moveaxis(v, 1, 0)
            S0 = jnp.zeros((B, H, D, D), x.dtype)
            z0 = jnp.zeros((B, H, D), x.dtype)

            def step(carry, inp):
                S, z = carry
                pq_t, pk_t, v_t = inp
                S = S + pk_t[..., :, None] * v_t[..., None, :]
                z = z + pk_t
                num = jnp.einsum('bhd,bhde->bhe', pq_t, S)
                den = jnp.sum(pq_t * z, axis=-1, keepdims=True) + EPS
                return ((S, z), num / den)
            (_, _), out = jax.lax.scan(step, (S0, z0), (pq, pk, vt))
            out = jnp.moveaxis(out, 0, 1).reshape(B, L, E)
            return out @ Wo.T + bo
        key = jax.random.key(seed)
        ks = jax.random.split(key, 6)
        B, L, E = (4, 2048, 512)
        s = 1.0 / np.sqrt(E)
        return {'x': jax.random.normal(ks[0], (B, L, E), jnp.float32), 'Wq': jax.random.normal(ks[1], (E, E), jnp.float32) * s, 'Wk': jax.random.normal(ks[2], (E, E), jnp.float32) * s, 'Wv': jax.random.normal(ks[3], (E, E), jnp.float32) * s, 'Wo': jax.random.normal(ks[4], (E, E), jnp.float32) * s, 'bo': jnp.zeros((E,), jnp.float32)}
    _L0_attn_in = _L0_attn_setup()

    def _L0_ffn_setup():
        import jax, jax.numpy as jnp
        import numpy as np
        S, B, D, H, DH = (2048, 8, 512, 16, 64)

        def _forward(x, Wg, Wq, bq, Wkv, bkv, Wo, bo, ln_g, ln_b):
            s_len, bsz, d_model = x.shape
            n_head, _, d_head = Wq.shape
            cap = s_len // n_head
            scale = 1.0 / d_head ** 0.5
            h = jnp.transpose(x, (1, 0, 2))
            t = h
            probs = jax.nn.softmax(h @ Wg, axis=-1)
            scores = jnp.transpose(probs, (0, 2, 1))
            _, idx = jax.lax.top_k(scores, cap)
            idx = jnp.sort(idx, axis=-1)
            hg = jnp.take_along_axis(h[:, None, :, :], idx[..., None], axis=2)
            hg = jnp.transpose(hg, (1, 0, 2, 3))
            q = jnp.einsum('hbcd,hde->hbce', hg, Wq) + bq[:, None, None, :]
            kv = jnp.einsum('hbcd,hde->hbce', hg, Wkv) + bkv[:, None, None, :]
            k, v = jnp.split(kv, 2, axis=-1)
            att = jnp.einsum('hbid,hbjd->hbij', q, k) * scale
            p = jax.nn.softmax(att, axis=1)
            av = jnp.einsum('hbij,hbjd->hbid', p, v)
            ao = jnp.einsum('hbid,hde->hbie', av, Wo) + bo
            tok = jnp.transpose(idx, (1, 0, 2))
            b_ids = jnp.arange(bsz)[None, :, None]
            outs = jnp.zeros_like(t).at[b_ids, tok].add(ao)
            y = t + outs
            mu = jnp.mean(y, axis=-1, keepdims=True)
            var = jnp.var(y, axis=-1, keepdims=True)
            yn = (y - mu) * jax.lax.rsqrt(var + 1e-05) * ln_g + ln_b
            return jnp.transpose(yn, (1, 0, 2))
        key = jax.random.key(seed)
        ks = jax.random.split(key, 6)
        s = 0.02
        return {'x': jax.random.normal(ks[0], (S, B, D), jnp.float32), 'attn_mask': jnp.zeros((S, S), jnp.bool_), 'Wg': jax.random.normal(ks[1], (D, H), jnp.float32) * s, 'Wq': jax.random.normal(ks[2], (H, D, DH), jnp.float32) * s, 'bq': jnp.zeros((H, DH), jnp.float32), 'Wkv': jax.random.normal(ks[3], (H, D, 2 * DH), jnp.float32) * s, 'bkv': jnp.zeros((H, 2 * DH), jnp.float32), 'Wo': jax.random.normal(ks[4], (H, DH, D), jnp.float32) * s, 'bo': jnp.zeros((D,), jnp.float32), 'ln_g': jnp.ones((D,), jnp.float32), 'ln_b': jnp.zeros((D,), jnp.float32)}
    _L0_ffn_in = _L0_ffn_setup()
    _d = {'L0_attn_x': _L0_attn_in['x'], 'L0_attn_Wq': _L0_attn_in['Wq'], 'L0_attn_Wk': _L0_attn_in['Wk'], 'L0_attn_Wv': _L0_attn_in['Wv'], 'L0_attn_Wo': _L0_attn_in['Wo'], 'L0_attn_bo': _L0_attn_in['bo'], 'L0_ffn_attn_mask': _L0_ffn_in['attn_mask'], 'L0_ffn_Wg': _L0_ffn_in['Wg'], 'L0_ffn_Wq': _L0_ffn_in['Wq'], 'L0_ffn_bq': _L0_ffn_in['bq'], 'L0_ffn_Wkv': _L0_ffn_in['Wkv'], 'L0_ffn_bkv': _L0_ffn_in['bkv'], 'L0_ffn_Wo': _L0_ffn_in['Wo'], 'L0_ffn_bo': _L0_ffn_in['bo'], 'L0_ffn_ln_g': _L0_ffn_in['ln_g'], 'L0_ffn_ln_b': _L0_ffn_in['ln_b']}
    _x0 = _d['L0_attn_x']
    _d['L0_attn_x'] = jax.random.normal(jax.random.fold_in(jax.random.key(seed), 1), (2, 4096, 512), dtype=_x0.dtype)
    del _x0
    return _d

def reference(L0_attn_x, L0_attn_Wq, L0_attn_Wk, L0_attn_Wv, L0_attn_Wo, L0_attn_bo, L0_ffn_attn_mask, L0_ffn_Wg, L0_ffn_Wq, L0_ffn_bq, L0_ffn_Wkv, L0_ffn_bkv, L0_ffn_Wo, L0_ffn_bo, L0_ffn_ln_g, L0_ffn_ln_b):

    def _L0_attn_ref(x, Wq, Wk, Wv, Wo, bo):
        import jax, jax.numpy as jnp
        import numpy as np
        EPS = 1e-05
        NUM_HEADS = 16

        def _linear_attention(x, Wq, Wk, Wv, Wo, bo):
            B, L, E = x.shape
            H = NUM_HEADS
            D = E // H
            q = (x @ Wq.T).reshape(B, L, H, D)
            k = (x @ Wk.T).reshape(B, L, H, D)
            v = (x @ Wv.T).reshape(B, L, H, D)
            phi_q = jax.nn.elu(q) + 1.0
            phi_k = jax.nn.elu(k) + 1.0
            pq = jnp.moveaxis(phi_q, 1, 0)
            pk = jnp.moveaxis(phi_k, 1, 0)
            vt = jnp.moveaxis(v, 1, 0)
            S0 = jnp.zeros((B, H, D, D), x.dtype)
            z0 = jnp.zeros((B, H, D), x.dtype)

            def step(carry, inp):
                S, z = carry
                pq_t, pk_t, v_t = inp
                S = S + pk_t[..., :, None] * v_t[..., None, :]
                z = z + pk_t
                num = jnp.einsum('bhd,bhde->bhe', pq_t, S)
                den = jnp.sum(pq_t * z, axis=-1, keepdims=True) + EPS
                return ((S, z), num / den)
            (_, _), out = jax.lax.scan(step, (S0, z0), (pq, pk, vt))
            out = jnp.moveaxis(out, 0, 1).reshape(B, L, E)
            return out @ Wo.T + bo
        return _linear_attention(x, Wq, Wk, Wv, Wo, bo)

    def _L0_ffn_ref(x, attn_mask, Wg, Wq, bq, Wkv, bkv, Wo, bo, ln_g, ln_b):
        import jax, jax.numpy as jnp
        import numpy as np
        S, B, D, H, DH = (2048, 8, 512, 16, 64)

        def _forward(x, Wg, Wq, bq, Wkv, bkv, Wo, bo, ln_g, ln_b):
            s_len, bsz, d_model = x.shape
            n_head, _, d_head = Wq.shape
            cap = s_len // n_head
            scale = 1.0 / d_head ** 0.5
            h = jnp.transpose(x, (1, 0, 2))
            t = h
            probs = jax.nn.softmax(h @ Wg, axis=-1)
            scores = jnp.transpose(probs, (0, 2, 1))
            _, idx = jax.lax.top_k(scores, cap)
            idx = jnp.sort(idx, axis=-1)
            hg = jnp.take_along_axis(h[:, None, :, :], idx[..., None], axis=2)
            hg = jnp.transpose(hg, (1, 0, 2, 3))
            q = jnp.einsum('hbcd,hde->hbce', hg, Wq) + bq[:, None, None, :]
            kv = jnp.einsum('hbcd,hde->hbce', hg, Wkv) + bkv[:, None, None, :]
            k, v = jnp.split(kv, 2, axis=-1)
            att = jnp.einsum('hbid,hbjd->hbij', q, k) * scale
            p = jax.nn.softmax(att, axis=1)
            av = jnp.einsum('hbij,hbjd->hbid', p, v)
            ao = jnp.einsum('hbid,hde->hbie', av, Wo) + bo
            tok = jnp.transpose(idx, (1, 0, 2))
            b_ids = jnp.arange(bsz)[None, :, None]
            outs = jnp.zeros_like(t).at[b_ids, tok].add(ao)
            y = t + outs
            mu = jnp.mean(y, axis=-1, keepdims=True)
            var = jnp.var(y, axis=-1, keepdims=True)
            yn = (y - mu) * jax.lax.rsqrt(var + 1e-05) * ln_g + ln_b
            return jnp.transpose(yn, (1, 0, 2))
        return _forward(x, Wg, Wq, bq, Wkv, bkv, Wo, bo, ln_g, ln_b)
    x = L0_attn_x
    x = x + 0.5 * _L0_ffn_ref(_layernorm(x, axis=-1), L0_ffn_attn_mask, L0_ffn_Wg, L0_ffn_Wq, L0_ffn_bq, L0_ffn_Wkv, L0_ffn_bkv, L0_ffn_Wo, L0_ffn_bo, L0_ffn_ln_g, L0_ffn_ln_b)
    x = x + _L0_attn_ref(_layernorm(x, axis=-1), L0_attn_Wq, L0_attn_Wk, L0_attn_Wv, L0_attn_Wo, L0_attn_bo)
    x = x + 0.5 * _L0_ffn_ref(_layernorm(x, axis=-1), L0_ffn_attn_mask, L0_ffn_Wg, L0_ffn_Wq, L0_ffn_bq, L0_ffn_Wkv, L0_ffn_bkv, L0_ffn_Wo, L0_ffn_bo, L0_ffn_ln_g, L0_ffn_ln_b)
    return x

_drawn_inputs = setup_inputs


def setup_inputs(seed=0):
    import zlib

    import numpy as np

    out = dict(_drawn_inputs(seed))
    spreads = {'L0_attn_bo': (0.0, 0.1),
     'L0_ffn_bq': (0.0, 0.1),
     'L0_ffn_bkv': (0.0, 0.1),
     'L0_ffn_bo': (0.0, 0.1),
     'L0_ffn_ln_g': (1.0, 0.2),
     'L0_ffn_ln_b': (0.0, 0.1)}
    factors = {}
    for name, (base, spread) in spreads.items():
        noise = np.random.default_rng([zlib.crc32(name.encode()), seed]).standard_normal(out[name].shape)
        drawn = base * np.exp(spread * noise) if base else spread * noise
        out[name] = jnp.asarray(drawn.astype(out[name].dtype))
    for name, factor in factors.items():
        out[name] = (out[name] * factor).astype(out[name].dtype)
    return out
```

```python
from contextlib import ExitStack

import concourse.bass as bass
from concourse import mybir

P = 128
BATCH, LEN, E = 2, 4096, 512
H, D = 16, 32
QUADS = P // D
GROUPS = E // P
C = 128
CHUNKS = LEN // C
DA = D + 1
TOK = BATCH * C
EPS = 1e-5

X_UP = 64.0
TOP = 2.0 ** 14
SUM_DOWN = 2.0 ** -27
V_SCALE = 2.0 ** -11
ATTN_UP = 2.0 ** 15

F32 = mybir.dt.float32
F16 = mybir.dt.float16
U32 = mybir.dt.uint32
ALU = mybir.AluOpType
ACT = mybir.ActivationFunctionType
RMAX = bass.bass_isa.ReduceOp.max

HI, LO = 0, 1
PASSES = ((HI, HI), (HI, LO), (LO, HI))
K_STACK = (HI, HI, LO)
Q_STACK = (HI, LO, HI)
STACK = len(K_STACK) * D
RESTACKS = QUADS * len(K_STACK)


class Signal:

    def __init__(self, sem, per, by=1, base=0):
        self.sem, self.per, self.by, self.base = sem, per, by, base

    def at(self, i, k=0):
        return i * (self.per * self.by) + (self.base + self.by * (k + 1))


def wait(eng, signal, i, k=0):
    if isinstance(i, int) and i < 0:
        return
    eng.wait_ge(signal.sem, signal.at(i, k))


def build(nc, x, Wq, Wk, Wv, Wo, attn_bo, ln_g, ln_b, out):
    with ExitStack() as ctx:
        def sb(name, shape, dt=F32):
            return ctx.enter_context(nc.sbuf_tensor(name, shape, dt))

        def ps(name, shape=(P, E), dt=F32):
            return ctx.enter_context(nc.psum_tensor(name, list(shape), dt))

        def sem(name):
            return ctx.enter_context(nc.semaphore(name))

        def sig(name, per, by=1, base=0):
            return Signal(sem(name), per, by, base)

        ident = sb("ident", [P, P])
        ident16 = sb("ident16", [P, P], F16)
        causal = sb("causal", [P, P])
        blocks = sb("blocks", [P, GROUPS // 2, QUADS, DA])
        gain = sb("gain", [P, E])
        shift = sb("shift", [P, BATCH, E])
        obias = sb("obias", [P, BATCH, E])
        neg_half = sb("neg_half", [P, BATCH])
        half4 = sb("half4", [P, 4])

        wT = [sb(f"wT{m}", [P, 2, GROUPS, E], F16) for m in range(4)]
        sumsq = sb("sumsq", [P, 4, GROUPS])
        norm2 = sb("norm2", [P, 4])
        norm2_all = sb("norm2_all", [P, 4])
        norm = sb("norm", [P, 4])
        pow2 = sb("pow2", [P, 4])
        rpow2 = sb("rpow2", [P, 4])
        w_scale = sb("w_scale", [P, 4])
        inv_scale = sb("inv_scale", [P, 2])
        f_bound = sb("f_bound", [P, 2])
        f_scale = sb("f_scale", [P, 2])
        den_eps = sb("den_eps", [P, 1])
        out_scale = sb("out_scale", [P, 1])

        X = sb("X", [P, 2, BATCH, E])
        XB = sb("XB", [P, BATCH, E])
        GAINED = sb("GAINED", [P, BATCH, E])
        X1 = sb("X1", [P, BATCH, E])
        X1BO = sb("X1BO", [P, 2, BATCH, E])
        XN = sb("XN", [P, BATCH, E])
        raw = sb("raw", [P, BATCH, 6])
        stat0 = sb("stat0", [P, BATCH, 2])
        stat1 = sb("stat1", [P, BATCH, 2])
        stat2 = sb("stat2", [P, BATCH, 2])
        var0 = sb("var0", [P, BATCH])
        var1 = sb("var1", [P, BATCH])
        var2 = sb("var2", [P, BATCH])
        rstd0 = sb("rstd0", [P, BATCH])
        rstd1 = sb("rstd1", [P, BATCH])
        rstd2 = sb("rstd2", [P, BATCH])
        XT = sb("XT", [P, 2, GROUPS, TOK], F16)
        EXPD = sb("EXPD", [P, 2, E])
        RELU = sb("RELU", [P, 2, E])
        PHIQ = sb("PHIQ", [P, 2, 2, TOK])
        PHIK = sb("PHIK", [P, BATCH, E])
        QT = [sb(f"QT{p}", [P, 2, GROUPS, TOK], F16) for p in range(2)]
        KT = sb("KT", [P, 2, GROUPS, TOK], F16)
        QS = [sb(f"QS{p}", [P, H, TOK], F16) for p in range(2)]
        KS = [sb(f"KS{p}", [P, H, TOK], F16) for p in range(2)]
        KN = [sb(f"KN{p}", [P, BATCH, 2, E], F16) for p in range(2)]
        VN = [sb(f"VN{p}", [P, BATCH, 2, H, DA], F16) for p in range(2)]
        AM = sb("AM", [P, 3, E])
        A = sb("A", [P, BATCH, 2, GROUPS, E], F16)
        wnat = [A[:, m].rearrange("p f g q -> p (f g q)").bitcast(F32).rearrange("p (c e) -> p c e", c=GROUPS)
                for m in range(2)]
        wnat += [QS[m][:].rearrange("p h t -> p (h t)").bitcast(F32).rearrange("p (c e) -> p c e", c=GROUPS)
                 for m in range(2)]
        DELTA = sb("DELTA", [P, 2, 2 * QUADS * DA])
        S = sb("S", [P, BATCH, 2, 2 * QUADS * DA])
        SH = sb("SH", [P, BATCH, 2, 2, 2 * QUADS * DA], F16)
        DEN = sb("DEN", [P, 2, H // 2])
        RDEN = sb("RDEN", [P, 2, H // 2])
        ATTN = sb("ATTN", [P, BATCH, E])
        AT = sb("AT", [P, BATCH, 2, E], F16)
        X2 = sb("X2", [P, BATCH, E])
        Y = sb("Y", [P, BATCH, E])
        raw2 = sb("raw2", [P, BATCH, 6])
        wsq = Y[:, 0]

        TP = [ps(f"TP{i}") for i in range(2)]
        PJ = [ps(f"PJ{i}") for i in range(2)]
        SC = [ps(f"SC{i}") for i in range(2)]
        AV = [ps(f"AV{i}") for i in range(2)]
        TP16 = [t[:].bitcast(F16) for t in TP]

        w_loaded = [sem(f"w_loaded{m}") for m in range(4)]
        consts_loaded = sem("consts_loaded")
        consts_done = sem("consts_done")
        pool_step = sem("pool_step")
        w_summed = sem("w_summed")
        norm2_done = sem("norm2_done")
        norm2_reduced = sem("norm2_reduced")
        norm_done = sem("norm_done")
        scales_done = sem("scales_done")
        dve_setup = sem("dve_setup")
        wT_filled = sem("wT_filled")
        wT_hi = sem("wT_hi")
        wT_lo = sem("wT_lo")
        consts_scaled = sem("consts_scaled")
        zeroed = sem("zeroed")

        x_loaded = [sem(f"x_loaded{p}") for p in range(2)]
        stat0_raw, stat0_done = sig("stat0_raw", 2), sig("stat0_done", 2)
        stat1_raw, stat1_done = sig("stat1_raw", 2), sig("stat1_done", 2)
        stat2_raw, stat2_done = sig("stat2_raw", 2), sig("stat2_done", 2)
        var0_done, var1_done, var2_done = sig("var0_done", 1), sig("var1_done", 1), sig("var2_done", 1)
        rstd0_done, rstd1_done, rstd2_done = sig("rstd0_done", 1), sig("rstd1_done", 1), sig("rstd2_done", 1)
        xb_done, x1bo_done, x2b_done = sig("xb_done", 1), sig("x1bo_done", 1), sig("x2b_done", 1)
        x_gained, x1_done, xn_done = sig("x_gained", 2), sig("x1_done", 2), sig("xn_done", 2)
        xT_filled, xT_hi, xT_lo = sig("xT_filled", 2), sig("xT_hi", 2), sig("xT_lo", 2)
        q_filled, q_exp, q_relu = sig("q_filled", 2), sig("q_exp", 2), sig("q_relu", 2)
        q_phi, q_hi, q_lo = sig("q_phi", 2), sig("q_hi", 2), sig("q_lo", 2)
        k_filled, k_exp, k_relu = sig("k_filled", 2), sig("k_exp", 2), sig("k_relu", 2)
        k_phi, k_hi, k_lo = sig("k_phi", 2), sig("k_hi", 2), sig("k_lo", 2)
        v_filled, v_hi, v_lo = sig("v_filled", 2), sig("v_hi", 2), sig("v_lo", 2)
        kT_filled, kT_copied = sig("kT_filled", 2), sig("kT_copied", 2)
        q_stacked = [sem(f"q_stacked{p}") for p in range(2)]
        k_stacked = [sem(f"k_stacked{p}") for p in range(2)]
        sc_filled, sc_masked = sig("sc_filled", 8), sig("sc_masked", 8)
        a_hi, a_lo = sig("a_hi", 8), sig("a_lo", 8)
        av_filled, den_done, rden_done, attn_done = (sig("av_filled", 4), sig("den_done", 4),
                                                     sig("rden_done", 4), sig("attn_done", 4))
        st_filled, delta_done = sig("st_filled", 4), sig("delta_done", 4)
        s_added, s_hi, s_lo = sig("s_added", 4), sig("s_hi", 2), sig("s_lo", 2)
        attnT_filled, attnT_hi, attnT_lo = sig("attnT_filled", 2), sig("attnT_hi", 2), sig("attnT_lo", 2)
        out_filled, x2_done = sig("out_filled", 2), sig("x2_done", 2)
        x2_gained, y_done = sig("x2_gained", 2), sig("y_done", 2)
        y_stored = sig("y_stored", 1, 16)

        def par_at(i, by):
            if isinstance(i, int):
                return (i // 2 + 1) * by
            raise AssertionError

        steps = CHUNKS
        weights = (Wq, Wk, Wv, Wo)

        class Step:

            def __init__(self, t, r):
                self.t, self.r = t, r
                self.number = isinstance(t, int)

            def chunk(self, ahead):
                return self.t * 2 + (self.r + ahead)

            def parity(self, ahead):
                return (self.r + ahead) % 2

            def pair(self, ahead, by):
                return self.t * by + ((self.r + ahead) // 2 + 1) * by

            def has(self, ahead):
                return not self.number or 0 <= self.chunk(ahead) < steps

        def run(eng, body):
            for s in range(-2, 2):
                body(Step(0, s))
            with eng.Fori(1, steps // 2 - 2) as t:
                body(Step(t, 0))
                body(Step(t, 1))
            for s in range(steps - 4, steps + 1):
                body(Step(0, s))

        def pair_wait(eng, sems, st, ahead, by):
            eng.wait_ge(sems[st.parity(ahead)], st.pair(ahead, by))

        passed = {e: sem(f"passed_{e}") for e in ("sp", "pool", "dve")}

        def stand(eng, name):
            eng.sem_inc(passed[name], 1)

        block = ctx.enter_context(nc.Block())

        @block.sync
        def _(sp):
            for m in range(4):
                sp.dma_start(wnat[m], weights[m].rearrange("(c p) e -> p c e", p=P)).then_inc(w_loaded[m], 16)
                if m == 0:
                    sp.dma_start(gain[:], ln_g.rearrange("(a n) -> a n", a=1).to_broadcast([P, E])).then_inc(consts_loaded, 16)
                    for b in range(BATCH):
                        sp.dma_start(shift[:, b], ln_b.rearrange("(a n) -> a n", a=1).to_broadcast([P, E])).then_inc(consts_loaded, 16)
                        sp.dma_start(obias[:, b], attn_bo.rearrange("(a n) -> a n", a=1).to_broadcast([P, E])).then_inc(consts_loaded, 16)
                if m == 1:
                    for i in range(2):
                        sp.dma_start(X[:, i], x[:, i * C:(i + 1) * C, :].rearrange("b p e -> p b e")).then_inc(x_loaded[i], 16)

            def body(st):
                n, p = st.chunk(1), st.parity(1)
                if st.has(4) and (not st.number or st.chunk(4) >= 2):
                    wait(sp, x_gained, st.chunk(2), 1)
                    stand(sp, "sp")
                    wait(sp, xb_done, st.chunk(2))
                    stand(sp, "sp")
                    i = st.chunk(4)
                    start = i * C
                    sp.dma_start(X[:, st.parity(4)], x[:, bass.ds(start, C), :].rearrange("b p e -> p b e")).then_inc(x_loaded[st.parity(4)], 16)
                if st.has(1):
                    wait(sp, q_hi, n, 1)
                    wait(sp, q_lo, n, 1)
                    if st.has(-1):
                        wait(sp, sc_filled, st.chunk(-1), 7)
                    for j, half in enumerate(Q_STACK):
                        for h in range(QUADS):
                            sp.dma_start(QS[p][D * j:D * j + D, h::QUADS, :],
                                         QT[p][D * h:D * h + D, half]).then_inc(q_stacked[p], 16)
                    wait(sp, kT_copied, n, 1)
                    for j, half in enumerate(K_STACK):
                        for h in range(QUADS):
                            sp.dma_start(KS[p][D * j:D * j + D, h::QUADS, :],
                                         KT[D * h:D * h + D, half]).then_inc(k_stacked[p], 16)
                if st.has(-1):
                    i = st.chunk(-1)
                    wait(sp, y_done, i, 1)
                    stand(sp, "sp")
                    sp.dma_start(out[:, bass.ds(i * C, C), :].rearrange("b p e -> p b e"), Y[:]).then_inc(y_stored.sem, 16)

            run(sp, body)
            wait(sp, y_stored, steps - 1)

        @block.gpsimd
        def _(pool):
            g = nc.gpsimd
            count = [0]

            def link(ins):
                count[0] += 1
                ins.then_inc(pool_step, 1)
                pool.wait_ge(pool_step, count[0])

            g.memset(neg_half[:], -0.5)
            g.memset(half4[:], 0.5)
            g.memset(ident[:], 0.0)
            link(g.memset(causal[:], SUM_DOWN))
            g.memset(blocks[:], SUM_DOWN)
            link(g.affine_select(out=ident[:], in_=ident[:], compare_op=ALU.not_equal, fill=1.0, base=0,
                                 pattern=[[-1, P]], channel_multiplier=1))
            link(g.affine_select(out=causal[:], in_=causal[:], compare_op=ALU.is_ge, fill=0.0, base=0,
                                 pattern=[[1, P]], channel_multiplier=-1))
            link(g.affine_select(out=blocks[:], in_=blocks[:], compare_op=ALU.is_ge, fill=0.0, base=0,
                                 pattern=[[0, 2], [-D, QUADS], [0, DA]], channel_multiplier=1))
            link(g.affine_select(out=blocks[:], in_=blocks[:], compare_op=ALU.is_ge, fill=0.0, base=D - 1,
                                 pattern=[[0, 2], [D, QUADS], [0, DA]], channel_multiplier=-1))
            g.tensor_copy(ident16[:], ident[:]).then_inc(consts_done, 1)
            pool.wait_ge(norm2_done, 1)
            g.partition_all_reduce(norm2_all[:], norm2[:], P, RMAX).then_inc(norm2_reduced, 1)
            pool.wait_ge(norm2_reduced, 1)
            g.tensor_tensor(norm[:], norm2_all[:], half4[:], ALU.pow).then_inc(norm_done, 1)
            pool.wait_ge(consts_scaled, 2)
            pool.wait_ge(scales_done, 1)
            pool.wait_ge(zeroed, 1)

            def rstd(var, var_done, rstd_, rstd_done, stat, stat_done, i, prev, double):
                if prev is not None:
                    wait(pool, rstd_done, prev)
                wait(pool, stat_done, i, 1)
                a, c = (1.0 + EPS, EPS * EPS) if double else (1.0, EPS)
                stand(pool, "pool")
                g.tensor_scalar(var[:], stat[:, :, 1], a, c, ALU.mult, ALU.add).then_inc(var_done.sem, 1)
                wait(pool, var_done, i)
                g.tensor_tensor(rstd_[:], var[:], neg_half[:], ALU.pow).then_inc(rstd_done.sem, 1)

            def body(st):
                s, n, f, back = st.chunk(0), st.chunk(1), st.chunk(2), st.chunk(-1)
                if st.has(1):
                    wait(pool, x1_done, n, 1)
                    if st.has(-1):
                        wait(pool, x2_done, back, 1)
                    g.tensor_tensor(X1BO[:, st.parity(1)], X1[:], obias[:], ALU.add).then_inc(x1bo_done.sem, 1)
                if st.has(2):
                    wait(pool, stat0_done, f, 1)
                    if st.has(1):
                        wait(pool, x1_done, n, 1)
                    rstd(var0, var0_done, rstd0, rstd0_done, stat0, stat0_done, f, n if st.has(1) else None, True)
                    g.tensor_tensor(XB[:], X[:, st.parity(2)], shift[:], ALU.add).then_inc(xb_done.sem, 1)
                if st.has(-1):
                    if st.has(-2):
                        wait(pool, y_done, st.chunk(-2), 1)
                    rstd(var2, var2_done, rstd2, rstd2_done, stat2, stat2_done, back, st.chunk(-2) if st.has(-2) else None, True)
                    wait(pool, x2_gained, back, 1)
                    g.tensor_tensor(X2[:], X2[:], shift[:], ALU.add).then_inc(x2b_done.sem, 1)

                def split_a(b, hg):
                    k = b * GROUPS + hg
                    wait(pool, a_hi, s, k)
                    g.tensor_tensor(A[:, b, LO, hg], AM[:, k % 2], A[:, b, HI, hg], ALU.subtract).then_inc(a_lo.sem, 1)

                def split_q(pr):
                    wait(pool, q_phi, n, pr)
                    if st.has(-1) and pr == 0:
                        wait(pool, av_filled, back, 3)
                        pair_wait(pool, q_stacked, st, -1, 16 * RESTACKS)
                    stand(pool, "pool")
                    g.tensor_scalar(QT[st.parity(1)][:, HI, 2 * pr:2 * pr + 2], PHIQ[:, pr], f_scale[:, 0:1], 1.0,
                                    ALU.mult, ALU.mult).then_inc(q_hi.sem, 1)

                def split_k(b):
                    wait(pool, k_phi, n, b)
                    if st.has(-1):
                        wait(pool, st_filled, back, 2 * b + 1)
                    stand(pool, "pool")
                    g.tensor_scalar(KN[st.parity(1)][:, b, HI], PHIK[:, b], f_scale[:, 1:2], 1.0,
                                    ALU.mult, ALU.mult).then_inc(k_hi.sem, 1)

                def add_s(b, hf):
                    wait(pool, delta_done, s, 2 * b + hf)
                    if hf == 0 and st.has(-1):
                        wait(pool, s_hi, back, b)
                        wait(pool, s_lo, back, b)
                    g.tensor_tensor(S[:, b, hf], S[:, b, hf], DELTA[:, hf], ALU.add).then_inc(s_added.sem, 1)

                def split_s(b):
                    wait(pool, s_hi, s, b)
                    g.tensor_tensor(SH[:, b, LO], S[:, b], SH[:, b, HI], ALU.subtract).then_inc(s_lo.sem, 1)

                if st.has(0):
                    split_a(0, 0)
                    split_a(0, 1)
                if st.has(1):
                    split_q(0)
                if st.has(0):
                    split_a(0, 2)
                    split_a(0, 3)
                if st.has(1):
                    split_q(1)
                    split_k(0)
                if st.has(0):
                    split_a(1, 0)
                    split_a(1, 1)
                if st.has(1):
                    split_k(1)
                if st.has(0):
                    split_a(1, 2)
                    split_a(1, 3)
                if st.has(2):
                    if st.has(1):
                        wait(pool, xn_done, n, 1)
                    rstd(var1, var1_done, rstd1, rstd1_done, stat1, stat1_done, f, n if st.has(1) else None, False)
                if st.has(0):
                    for b in range(BATCH):
                        add_s(b, 0)
                        add_s(b, 1)
                        split_s(b)

            run(pool, body)

        @block.scalar
        def _(act):
            a = nc.scalar
            for m in range(4):
                act.wait_ge(w_loaded[m], 16)
                for c in range(GROUPS):
                    ins = a.activation(wsq, wnat[m][:, c], ACT.Square, accum_out=sumsq[:, m, c:c + 1])
                    ins.then_inc(w_summed, 1)
                    act.wait_ge(w_summed, m * GROUPS + c + 1)
            act.wait_ge(scales_done, 1)
            for m in range(4):
                for c in range(GROUPS):
                    k = m * GROUPS + c
                    act.wait_ge(wT_filled, k + 1)
                    a.activation(wT[m][:, HI, c], TP[c % 2][:], ACT.Copy, scale=w_scale[:, m:m + 1]).then_inc(wT_hi, 1)

            def exp_relu(bank, slot, scale, filled, exp_done, relu_done, phi_done, i, k, started):
                wait(act, filled, i, k)
                if started:
                    phi_done()
                a.activation(EXPD[:, slot], bank[:], ACT.Exp, scale=scale).then_inc(exp_done.sem, 1)
                a.activation(RELU[:, slot], bank[:], ACT.Relu, scale=scale).then_inc(relu_done.sem, 1)

            def body(st):
                s, n, back = st.chunk(0), st.chunk(1), st.chunk(-1)

                def x_halves(b):
                    wait(act, xT_filled, n, b)
                    if st.has(0):
                        wait(act, v_filled, s, 1)
                    a.activation(XT[:, HI, :, b * C:(b + 1) * C], TP[b][:].rearrange("p (c t) -> p c t", c=GROUPS),
                                 ACT.Copy, scale=X_UP).then_inc(xT_hi.sem, 1)

                def split_a(b, hg):
                    k = b * GROUPS + hg
                    wait(act, sc_masked, s, k)
                    if hg == 0 and st.has(-1):
                        wait(act, av_filled, back, 2 * b + 1)
                    a.activation(A[:, b, HI, hg], AM[:, k % 2], ACT.Copy).then_inc(a_hi.sem, 1)

                def kT(b):
                    wait(act, kT_filled, n, b)
                    if st.has(0) and b == 0:
                        pair_wait(act, k_stacked, st, 0, 16 * RESTACKS)
                    a.activation(KT[:, :, :, b * C:(b + 1) * C],
                                 TP16[b].rearrange("p (f c t) -> p f c t", f=2, c=GROUPS),
                                 ACT.Copy).then_inc(kT_copied.sem, 1)

                def v_half(b):
                    wait(act, v_filled, n, b)
                    if st.has(-1):
                        wait(act, st_filled, back, 2 * b + 1)
                    a.activation(VN[st.parity(1)][:, b, HI, :, 0:D], PJ[b][:].rearrange("p (h d) -> p h d", h=H),
                                 ACT.Copy, scale=V_SCALE).then_inc(v_hi.sem, 1)

                def attn_half(b):
                    wait(act, attnT_filled, s, b)
                    if st.has(-1):
                        wait(act, out_filled, back, b)
                    a.activation(AT[:, b, HI], TP[b][:], ACT.Copy, scale=ATTN_UP).then_inc(attnT_hi.sem, 1)

                def s_half(b):
                    wait(act, s_added, s, 2 * b + 1)
                    wait(act, av_filled, s, 2 * b + 1)
                    a.activation(SH[:, b, HI], S[:, b], ACT.Copy).then_inc(s_hi.sem, 1)

                A_, B_ = st.has(1), st.has(0)
                if A_:
                    x_halves(0)
                    x_halves(1)
                if B_:
                    split_a(0, 0)
                    split_a(0, 1)
                if A_:
                    exp_relu(PJ[0], 0, inv_scale[:, 0:1], q_filled, q_exp, q_relu,
                             lambda: wait(act, k_phi, s, 0), n, 0, st.has(0))
                if B_:
                    split_a(0, 2)
                    split_a(0, 3)
                if A_:
                    exp_relu(PJ[1], 1, inv_scale[:, 0:1], q_filled, q_exp, q_relu,
                             lambda: wait(act, k_phi, s, 1), n, 1, st.has(0))
                    exp_relu(PJ[0], 0, inv_scale[:, 1:2], k_filled, k_exp, k_relu,
                             lambda: wait(act, q_phi, n, 0), n, 0, True)
                if B_:
                    split_a(1, 0)
                    split_a(1, 1)
                if A_:
                    exp_relu(PJ[1], 1, inv_scale[:, 1:2], k_filled, k_exp, k_relu,
                             lambda: wait(act, q_phi, n, 1), n, 1, True)
                if B_:
                    split_a(1, 2)
                    split_a(1, 3)
                if A_:
                    v_half(0)
                    kT(0)
                    v_half(1)
                    kT(1)
                if B_:
                    s_half(0)
                    attn_half(0)
                    s_half(1)
                    attn_half(1)

            run(act, body)

        @block.vector
        def _(dve):
            v = nc.vector
            count = [0]

            def link(ins):
                count[0] += 1
                ins.then_inc(dve_setup, 1)
                dve.wait_ge(dve_setup, count[0])

            link(v.memset(S[:], 0.0))
            link(v.memset(SH[:], 0.0))
            for p in range(2):
                link(v.memset(VN[p][:, :, HI, :, D:DA], ATTN_UP))
                link(v.memset(VN[p][:, :, LO, :, D:DA], 0.0))
            dve.wait_ge(consts_loaded, 16 * (1 + 2 * BATCH))
            v.tensor_scalar(gain[:], gain[:], 0.5, None, ALU.mult).then_inc(consts_scaled, 1)
            v.tensor_scalar(shift[:], shift[:], 0.5, None, ALU.mult).then_inc(consts_scaled, 1)
            dve.wait_ge(consts_scaled, 2)
            dve.wait_ge(w_summed, 4 * GROUPS)
            link(v.tensor_reduce(norm2[:], sumsq[:], mybir.AxisListType.X, ALU.max))
            v.tensor_scalar(norm2[:], norm2[:], 1e-30, None, ALU.max).then_inc(norm2_done, 1)
            dve.wait_ge(norm_done, 1)
            link(v.tensor_scalar(pow2[:].bitcast(U32), norm[:].bitcast(U32), 0x7F800000, None, ALU.bitwise_and))
            link(v.reciprocal(rpow2[:], pow2[:]))
            link(v.tensor_scalar(w_scale[:], rpow2[:], TOP, None, ALU.mult))
            link(v.tensor_scalar(inv_scale[:], pow2[:, 0:2], 1.0 / (TOP * X_UP), None, ALU.mult))
            link(v.tensor_scalar(f_bound[:], pow2[:, 0:2], 64.0, 1.0, ALU.mult, ALU.max))
            link(v.reciprocal(f_scale[:], f_bound[:]))
            link(v.tensor_scalar(f_scale[:], f_scale[:], TOP, None, ALU.mult))
            link(v.tensor_tensor(den_eps[:], f_scale[:, 0:1], f_scale[:, 1:2], ALU.mult))
            link(v.tensor_scalar(den_eps[:], den_eps[:], SUM_DOWN * ATTN_UP, EPS, ALU.mult, ALU.mult))
            link(v.tensor_tensor(out_scale[:], pow2[:, 2:3], pow2[:, 3:4], ALU.mult))
            v.tensor_scalar(out_scale[:], out_scale[:], 1.0 / (TOP * X_UP * V_SCALE * TOP), None, ALU.mult).then_inc(scales_done, 1)
            dve.wait_ge(scales_done, 1)
            for m in range(4):
                for c in range(GROUPS):
                    k = m * GROUPS + c
                    dve.wait_ge(wT_hi, k + 1)
                    v.scalar_tensor_tensor(wT[m][:, LO, c], TP[c % 2][:], w_scale[:, m:m + 1], wT[m][:, HI, c],
                                           ALU.mult, ALU.subtract).then_inc(wT_lo, 1)
            dve.wait_ge(wT_lo, 4 * GROUPS)
            v.memset(raw[:], 0.0).then_inc(zeroed, 1)
            dve.wait_ge(zeroed, 1)
            dve.wait_ge(consts_done, 1)

            def stats(src, rawt, stat, raw_sig, done_sig, i, b):
                v.bn_stats(rawt[:, b], src).then_inc(raw_sig.sem, 1)
                wait(dve, raw_sig, i, b)
                stand(dve, "dve")
                v.bn_aggr(stat[:, b], rawt[:, b]).then_inc(done_sig.sem, 1)

            def body(st):
                s, n, f, back = st.chunk(0), st.chunk(1), st.chunk(2), st.chunk(-1)
                A_, B_, F_, K_ = st.has(1), st.has(0), st.has(2), st.has(-1)

                def front_stats(b):
                    if b == 0:
                        pair_wait(dve, x_loaded, st, 2, 16)
                        if st.has(1):
                            wait(dve, var0_done, n)
                            wait(dve, x_gained, n, 1)
                            wait(dve, stat1_done, n, 1)
                    stats(X[:, st.parity(2), b], raw, stat0, stat0_raw, stat0_done, f, b)

                def front_gain(b):
                    if K_:
                        wait(dve, y_done, back, b)
                    v.scalar_tensor_tensor(GAINED[:, b], X[:, st.parity(2), b], stat0[:, b, 0:1], gain[:],
                                           ALU.subtract, ALU.mult).then_inc(x_gained.sem, 1)

                def front_x1(b):
                    wait(dve, x_gained, f, b)
                    if b == 0:
                        wait(dve, rstd0_done, f)
                        wait(dve, xb_done, f)
                        if st.has(1):
                            wait(dve, x1bo_done, n)
                            wait(dve, xn_done, n, 1)
                    v.scalar_tensor_tensor(X1[:, b], GAINED[:, b], rstd0[:, b:b + 1], XB[:, b],
                                           ALU.mult, ALU.add).then_inc(x1_done.sem, 1)

                def front_stats1(b):
                    wait(dve, x1_done, f, b)
                    if b == 0 and st.has(1):
                        wait(dve, var1_done, n)
                    stats(X1[:, b], raw, stat1, stat1_raw, stat1_done, f, b)

                def front_norm(b):
                    if b == 0:
                        wait(dve, rstd1_done, f)
                        if st.has(1):
                            wait(dve, xT_filled, n, 1)
                    v.tensor_scalar(XN[:, b], X1[:, b], stat1[:, b, 0:1], rstd1[:, b:b + 1],
                                    ALU.subtract, ALU.mult).then_inc(xn_done.sem, 1)

                def x_low(b):
                    wait(dve, xT_hi, n, b)
                    v.scalar_tensor_tensor(XT[:, LO, :, b * C:(b + 1) * C],
                                           TP[b][:].rearrange("p (c t) -> p c t", c=GROUPS), X_UP,
                                           XT[:, HI, :, b * C:(b + 1) * C],
                                           ALU.mult, ALU.subtract).then_inc(xT_lo.sem, 1)

                def mask(b, hg):
                    k = b * GROUPS + hg
                    wait(dve, sc_filled, s, k)
                    if k >= 2:
                        wait(dve, a_lo, s, k - 2)
                    elif K_:
                        wait(dve, a_lo, back, k + 6)
                    v.tensor_tensor(AM[:, k % 2].rearrange("p (h q) -> p h q", h=QUADS),
                                    SC[hg % 2][:].rearrange("p (h q) -> p h q", h=QUADS),
                                    causal[:].unsqueeze(1).to_broadcast([P, QUADS, C]),
                                    ALU.mult).then_inc(sc_masked.sem, 1)

                def phi_q(pr):
                    wait(dve, q_relu, n, pr)
                    if B_:
                        wait(dve, q_hi, s, pr)
                        wait(dve, q_lo, s, pr)
                    v.scalar_tensor_tensor(PHIQ[:, pr].rearrange("p g t -> p (g t)"), EXPD[:, pr], 1.0, RELU[:, pr],
                                           ALU.min, ALU.add).then_inc(q_phi.sem, 1)

                def low_q(pr):
                    wait(dve, q_hi, n, pr)
                    v.scalar_tensor_tensor(QT[st.parity(1)][:, LO, 2 * pr:2 * pr + 2], PHIQ[:, pr], f_scale[:, 0:1],
                                           QT[st.parity(1)][:, HI, 2 * pr:2 * pr + 2],
                                           ALU.mult, ALU.subtract).then_inc(q_lo.sem, 1)

                def phi_k(b):
                    wait(dve, k_relu, n, b)
                    if B_:
                        wait(dve, k_hi, s, b)
                        wait(dve, k_lo, s, b)
                    v.scalar_tensor_tensor(PHIK[:, b], EXPD[:, b], 1.0, RELU[:, b],
                                           ALU.min, ALU.add).then_inc(k_phi.sem, 1)

                def low_k(b):
                    wait(dve, k_hi, n, b)
                    v.scalar_tensor_tensor(KN[st.parity(1)][:, b, LO], PHIK[:, b], f_scale[:, 1:2],
                                           KN[st.parity(1)][:, b, HI], ALU.mult, ALU.subtract).then_inc(k_lo.sem, 1)

                def low_v(b):
                    wait(dve, v_hi, n, b)
                    v.scalar_tensor_tensor(VN[st.parity(1)][:, b, LO, :, 0:D], PJ[b][:].rearrange("p (h d) -> p h d", h=H),
                                           V_SCALE, VN[st.parity(1)][:, b, HI, :, 0:D],
                                           ALU.mult, ALU.subtract).then_inc(v_lo.sem, 1)

                def quotient(b, hf):
                    k = 2 * b + hf
                    wait(dve, av_filled, s, k)
                    av = AV[hf][:, 0:2 * QUADS * DA].rearrange("p (h d) -> p h d", d=DA)
                    if b == 1:
                        wait(dve, attn_done, s, hf)
                    elif K_:
                        wait(dve, attn_done, back, 2 + hf)
                    v.tensor_scalar(DEN[:, hf], av[:, :, D], den_eps[:], None, ALU.add).then_inc(den_done.sem, 1)
                    wait(dve, den_done, s, k)
                    v.reciprocal(RDEN[:, hf], DEN[:, hf]).then_inc(rden_done.sem, 1)
                    wait(dve, rden_done, s, k)
                    if K_ and hf == 0:
                        wait(dve, attnT_filled, back, b)
                    v.tensor_tensor(ATTN[:, b, hf * (E // 2):(hf + 1) * (E // 2)].rearrange("p (h d) -> p h d", d=D),
                                    av[:, :, 0:D], RDEN[:, hf].unsqueeze(2).to_broadcast([P, H // 2, D]),
                                    ALU.mult).then_inc(attn_done.sem, 1)

                def delta(b, hf):
                    k = 2 * b + hf
                    wait(dve, st_filled, s, k)
                    if b == 1:
                        wait(dve, s_added, s, hf)
                    elif K_:
                        wait(dve, s_added, back, 2 + hf)
                    v.tensor_tensor(DELTA[:, hf], PJ[(b + 1 + hf) % 2][:, 0:2 * QUADS * DA],
                                    blocks[:].rearrange("p g h d -> p (g h d)"), ALU.mult).then_inc(delta_done.sem, 1)

                def attn_low(b):
                    wait(dve, attnT_hi, s, b)
                    v.scalar_tensor_tensor(AT[:, b, LO], TP[b][:], ATTN_UP, AT[:, b, HI],
                                           ALU.mult, ALU.subtract).then_inc(attnT_lo.sem, 1)

                def add_out(b):
                    wait(dve, out_filled, s, b)
                    if b == 0:
                        wait(dve, x1bo_done, s)
                        if K_:
                            wait(dve, y_done, back, 1)
                            wait(dve, var2_done, back)
                    v.scalar_tensor_tensor(X2[:, b], PJ[b][:], out_scale[:], X1BO[:, st.parity(0), b],
                                           ALU.mult, ALU.add).then_inc(x2_done.sem, 1)
                    wait(dve, x2_done, s, b)
                    stats(X2[:, b], raw2, stat2, stat2_raw, stat2_done, s, b)

                def back_gain(b):
                    if A_:
                        wait(dve, x1_done, n, b)
                    v.scalar_tensor_tensor(GAINED[:, b], X2[:, b], stat2[:, b, 0:1], gain[:],
                                           ALU.subtract, ALU.mult).then_inc(x2_gained.sem, 1)

                def back_y(b):
                    wait(dve, x2_gained, back, b)
                    if b == 0:
                        wait(dve, rstd2_done, back)
                        wait(dve, x2b_done, back)
                        if st.has(-2):
                            wait(dve, y_stored, st.chunk(-2))
                    v.scalar_tensor_tensor(Y[:, b], GAINED[:, b], rstd2[:, b:b + 1], X2[:, b],
                                           ALU.mult, ALU.add).then_inc(y_done.sem, 1)

                def both(on, fn, *args):
                    if on:
                        for b in range(BATCH):
                            fn(b, *args)

                both(A_, x_low)
                if K_:
                    wait(dve, stat2_done, back, 1)
                both(K_, back_gain)
                if B_:
                    mask(0, 0)
                    mask(0, 1)
                both(F_, front_stats)
                if F_:
                    wait(dve, stat0_done, f, 1)
                if A_:
                    phi_q(0)
                if B_:
                    mask(0, 2)
                    mask(0, 3)
                both(K_, back_y)
                both(F_, front_gain)
                if A_:
                    phi_q(1)
                    low_q(0)
                    phi_k(0)
                    low_q(1)
                if B_:
                    mask(1, 0)
                    mask(1, 1)
                    quotient(0, 0)
                if A_:
                    low_k(0)
                    phi_k(1)
                both(F_, front_x1)
                if B_:
                    mask(1, 2)
                    mask(1, 3)
                    quotient(0, 1)
                both(F_, front_stats1)
                if A_:
                    low_k(1)
                    low_v(0)
                if B_:
                    quotient(1, 0)
                    delta(0, 0)
                    delta(0, 1)
                if A_:
                    low_v(1)
                if B_:
                    quotient(1, 1)
                both(F_, front_norm)
                if B_:
                    attn_low(0)
                    delta(1, 0)
                    delta(1, 1)
                    attn_low(1)
                    add_out(0)
                    add_out(1)

            run(dve, body)

        @block.tensor
        def _(pe):
            t_ = nc.tensor
            pe.wait_ge(consts_done, 1)
            for m in range(4):
                pe.wait_ge(w_loaded[m], 16)
                for c in range(GROUPS):
                    k = m * GROUPS + c
                    if k >= 2:
                        pe.wait_ge(wT_lo, k - 1)
                    for o in range(GROUPS):
                        ins = t_.transpose(TP[c % 2][:, o * P:(o + 1) * P], wnat[m][:, o, c * P:(c + 1) * P], ident[:])
                    ins.then_inc(wT_filled, 1)
            pe.wait_ge(wT_lo, 4 * GROUPS)
            pe.wait_ge(zeroed, 1)

            def body(st):
                s, n, back = st.chunk(0), st.chunk(1), st.chunk(-1)
                A_, B_, K_ = st.has(1), st.has(0), st.has(-1)
                cur, nxt = st.parity(0), st.parity(1)

                def x_transposes(b):
                    wait(pe, xn_done, n, b)
                    if K_:
                        wait(pe, attnT_lo, back, b)
                    elif B_:
                        wait(pe, kT_copied, s, b)
                    for c in range(GROUPS):
                        ins = t_.transpose(TP[b][:, c * P:(c + 1) * P], XN[:, b, c * P:(c + 1) * P], ident[:])
                    ins.then_inc(xT_filled.sem, 1)

                def bank_free(b):
                    if K_:
                        wait(pe, x2_done, back, b)
                    elif B_:
                        wait(pe, v_lo, s, b)

                def project_q(pr):
                    if pr == 0:
                        wait(pe, xT_lo, n, 1)
                    bank_free(pr)
                    for g in range(2):
                        fb = 2 * pr + g
                        todo = [(c, w, m) for c in range(GROUPS) for w, m in PASSES]
                        for c, w, m in todo:
                            ins = t_.matmul(PJ[pr][:, g * TOK:(g + 1) * TOK], wT[0][:, w, c, fb * P:(fb + 1) * P],
                                            XT[:, m, c, :], start=(c, w, m) == todo[0], stop=(c, w, m) == todo[-1])
                    ins.then_inc(q_filled.sem, 1)

                def project(m_, b, filled, k):
                    todo = [(c, w, m) for c in range(GROUPS) for w, m in PASSES]
                    for c, w, m in todo:
                        ins = t_.matmul(PJ[b][:], XT[:, w, c, b * C:(b + 1) * C], wT[m_][:, m, c, :],
                                        start=(c, w, m) == todo[0], stop=(c, w, m) == todo[-1])
                    ins.then_inc(filled.sem, 1)

                def k_transposes(b):
                    wait(pe, k_lo, n, b)
                    wait(pe, xT_lo, n, b)
                    for half in (HI, LO):
                        for c in range(GROUPS):
                            at = (half * GROUPS + c) * P
                            ins = t_.transpose(TP16[b][:, at:at + P], KN[nxt][:, b, half, c * P:(c + 1) * P], ident16[:])
                    ins.then_inc(kT_filled.sem, 1)

                def scores(b, hg):
                    k = b * GROUPS + hg
                    if k == 0:
                        pair_wait(pe, q_stacked, st, 0, 16 * RESTACKS)
                        pair_wait(pe, k_stacked, st, 0, 16 * RESTACKS)
                    if k >= 2:
                        wait(pe, sc_masked, s, k - 2)
                    elif K_:
                        wait(pe, sc_masked, back, k + 6)
                    for h in range(QUADS):
                        head = hg * QUADS + h
                        ins = t_.matmul(SC[hg % 2][:, h * C:(h + 1) * C], KS[cur][0:STACK, head, b * C:(b + 1) * C],
                                        QS[cur][0:STACK, head, b * C:(b + 1) * C], start=True, stop=True)
                    ins.then_inc(sc_filled.sem, 1)

                def attend(b, hf):
                    wait(pe, a_lo, s, b * GROUPS + 2 * hf + 1)
                    if K_ and hf == 0:
                        wait(pe, s_lo, back, b)
                    if b == 1:
                        wait(pe, attn_done, s, hf)
                    elif K_:
                        wait(pe, attn_done, back, 2 + hf)
                    for g in range(2):
                        hg = 2 * hf + g
                        w_ = QUADS * DA
                        for w, m in PASSES:
                            t_.matmul(AV[hf][:, g * w_:(g + 1) * w_], QT[cur][:, w, hg, b * C:(b + 1) * C],
                                      SH[:, b, m, hf, g * w_:(g + 1) * w_], start=(w, m) == PASSES[0], stop=False)
                        for h in range(QUADS):
                            for w, m in PASSES:
                                ins = t_.matmul(AV[hf][:, g * w_ + h * DA:g * w_ + (h + 1) * DA],
                                                A[:, b, w, hg, h * C:(h + 1) * C], VN[cur][:, b, m, hg * QUADS + h, :],
                                                start=False, stop=(h == QUADS - 1 and (w, m) == PASSES[-1]))
                    ins.then_inc(av_filled.sem, 1)

                def update(b, hf):
                    bank = (b + 1 + hf) % 2
                    w_ = QUADS * DA
                    for g in range(2):
                        hg = 2 * hf + g
                        for w, m in PASSES:
                            ins = t_.matmul(PJ[bank][:, g * w_:(g + 1) * w_], KN[cur][:, b, w, hg * P:(hg + 1) * P],
                                            VN[cur][:, b, m, hg * QUADS:(hg + 1) * QUADS, :],
                                            start=(w, m) == PASSES[0], stop=(w, m) == PASSES[-1])
                    ins.then_inc(st_filled.sem, 1)

                def attn_transposes(b):
                    wait(pe, attn_done, s, 2 * b + 1)
                    if A_:
                        wait(pe, kT_copied, n, b)
                    else:
                        wait(pe, attnT_lo, back, b)
                    for c in range(GROUPS):
                        ins = t_.transpose(TP[b][:, c * P:(c + 1) * P], ATTN[:, b, c * P:(c + 1) * P], ident[:])
                    ins.then_inc(attnT_filled.sem, 1)

                def project_out(b):
                    wait(pe, attnT_lo, s, b)
                    wait(pe, delta_done, s, 2 + b)
                    todo = [(c, w, m) for c in range(GROUPS) for w, m in PASSES]
                    for c, w, m in todo:
                        ins = t_.matmul(PJ[b][:], AT[:, b, w, c * C:(c + 1) * C], wT[3][:, m, c, :],
                                        start=(c, w, m) == todo[0], stop=(c, w, m) == todo[-1])
                    ins.then_inc(out_filled.sem, 1)

                if A_:
                    x_transposes(0)
                    x_transposes(1)
                if B_:
                    scores(0, 0)
                    scores(0, 1)
                if A_:
                    project_q(0)
                if B_:
                    scores(0, 2)
                    scores(0, 3)
                if A_:
                    project_q(1)
                    wait(pe, q_relu, n, 0)
                    project(1, 0, k_filled, 0)
                if B_:
                    attend(0, 0)
                    scores(1, 0)
                    scores(1, 1)
                if A_:
                    wait(pe, q_relu, n, 1)
                    project(1, 1, k_filled, 1)
                if B_:
                    attend(0, 1)
                    scores(1, 2)
                    scores(1, 3)
                if A_:
                    wait(pe, k_relu, n, 0)
                    project(2, 0, v_filled, 0)
                    k_transposes(0)
                if B_:
                    attend(1, 0)
                    if A_:
                        wait(pe, k_relu, n, 1)
                    else:
                        wait(pe, x2_done, back, 1)
                    update(0, 0)
                    if A_:
                        wait(pe, v_lo, n, 0)
                    else:
                        wait(pe, x2_done, back, 0)
                    update(0, 1)
                if A_:
                    if B_:
                        wait(pe, delta_done, s, 0)
                    else:
                        wait(pe, k_relu, n, 1)
                    project(2, 1, v_filled, 1)
                    k_transposes(1)
                if B_:
                    attend(1, 1)
                    attn_transposes(0)
                    wait(pe, delta_done, s, 1)
                    update(1, 0)
                    if A_:
                        wait(pe, v_lo, n, 1)
                    else:
                        wait(pe, delta_done, s, 0)
                    update(1, 1)
                    project_out(0)
                    attn_transposes(1)
                    project_out(1)

            run(pe, body)


_INS = ['L0_attn_x', 'L0_attn_Wq', 'L0_attn_Wk', 'L0_attn_Wv', 'L0_attn_Wo', 'L0_attn_bo', 'L0_ffn_ln_g', 'L0_ffn_ln_b']
_OUTS = [((BATCH, LEN, E), 'float32')]


def kernel(**inputs):
    import numpy as _np
    import concourse.bacc as _bacc
    from concourse import mybir as _mybir
    from concourse.bass_utils import run_bass_kernel_spmd as _run

    nc = _bacc.Bacc("TRN2", target_bir_lowering=False, num_devices=1)
    arrays, args = {}, []
    for name in _INS:
        a = _np.ascontiguousarray(inputs[name])
        arrays[f"in_{name}_dram"] = a
        args.append(nc.dram_tensor(f"in_{name}_dram", a.shape, _mybir.dt.from_np(a.dtype), kind="ExternalInput").ap())
    for i, (shape, dtype) in enumerate(_OUTS):
        dt = _mybir.dt.from_np(_np.dtype(dtype))
        args.append(nc.dram_tensor(f"out_{i}_dram", shape, dt, kind="ExternalOutput").ap())
    build(nc, *args)
    r = _run(nc, [arrays], core_ids=[0])
    got = tuple(r.results[0][f"out_{i}_dram"] for i in range(len(_OUTS)))
    return got[0]
```

```python
from contextlib import ExitStack

import concourse.bass as bass
from concourse import mybir

P = 128
BATCH, LEN, E = 2, 4096, 512
H, D = 16, 32
QUADS = P // D
GROUPS = E // P
C = 128
CHUNKS = LEN // C
DA = D + 1
TOK = BATCH * C
EPS = 1e-5

X_UP = 64.0
TOP = 2.0 ** 14
SUM_DOWN = 2.0 ** -27
V_SCALE = 2.0 ** -11
ATTN_UP = 2.0 ** 15

F32 = mybir.dt.float32
F16 = mybir.dt.float16
U32 = mybir.dt.uint32
ALU = mybir.AluOpType
ACT = mybir.ActivationFunctionType
RMAX = bass.bass_isa.ReduceOp.max

HI, LO = 0, 1
PASSES = ((HI, HI), (HI, LO), (LO, HI))
K_STACK = (HI, HI, LO)
Q_STACK = (HI, LO, HI)
STACK = len(K_STACK) * D
RESTACKS = QUADS * len(K_STACK)


class Signal:

    def __init__(self, sem, per, by=1, base=0):
        self.sem, self.per, self.by, self.base = sem, per, by, base

    def at(self, i, k=0):
        return i * (self.per * self.by) + (self.base + self.by * (k + 1))


def wait(eng, signal, i, k=0):
    if isinstance(i, int) and i < 0:
        return
    eng.wait_ge(signal.sem, signal.at(i, k))


def build(nc, x, Wq, Wk, Wv, Wo, attn_bo, ln_g, ln_b, out):
    with ExitStack() as ctx:
        def sb(name, shape, dt=F32):
            return ctx.enter_context(nc.sbuf_tensor(name, shape, dt))

        def ps(name, shape=(P, E), dt=F32):
            return ctx.enter_context(nc.psum_tensor(name, list(shape), dt))

        def sem(name):
            return ctx.enter_context(nc.semaphore(name))

        def sig(name, per, by=1, base=0):
            return Signal(sem(name), per, by, base)

        ident = sb("ident", [P, P])
        ident16 = sb("ident16", [P, P], F16)
        causal = sb("causal", [P, P])
        blocks = sb("blocks", [P, GROUPS // 2, QUADS, DA])
        gain = sb("gain", [P, E])
        shift = sb("shift", [P, BATCH, E])
        obias = sb("obias", [P, BATCH, E])
        neg_half = sb("neg_half", [P, BATCH])
        half4 = sb("half4", [P, 4])

        wT = [sb(f"wT{m}", [P, 2, GROUPS, E], F16) for m in range(4)]
        sumsq = sb("sumsq", [P, 4, GROUPS])
        norm2 = sb("norm2", [P, 4])
        norm2_all = sb("norm2_all", [P, 4])
        norm = sb("norm", [P, 4])
        pow2 = sb("pow2", [P, 4])
        rpow2 = sb("rpow2", [P, 4])
        w_scale = sb("w_scale", [P, 4])
        inv_scale = sb("inv_scale", [P, 2])
        f_bound = sb("f_bound", [P, 2])
        f_scale = sb("f_scale", [P, 2])
        den_eps = sb("den_eps", [P, 1])
        out_scale = sb("out_scale", [P, 1])

        X = sb("X", [P, 2, BATCH, E])
        XB = sb("XB", [P, BATCH, E])
        GAINED = sb("GAINED", [P, BATCH, E])
        X1 = sb("X1", [P, BATCH, E])
        X1BO = sb("X1BO", [P, 2, BATCH, E])
        XN = sb("XN", [P, BATCH, E])
        raw = sb("raw", [P, BATCH, 6])
        stat0 = sb("stat0", [P, BATCH, 2])
        stat1 = sb("stat1", [P, BATCH, 2])
        stat2 = sb("stat2", [P, BATCH, 2])
        var0 = sb("var0", [P, BATCH])
        var1 = sb("var1", [P, BATCH])
        var2 = sb("var2", [P, BATCH])
        rstd0 = sb("rstd0", [P, BATCH])
        rstd1 = sb("rstd1", [P, BATCH])
        rstd2 = sb("rstd2", [P, BATCH])
        minus_one = sb("minus_one", [P, BATCH])
        neg_mean = sb("neg_mean", [P, BATCH])
        offset1 = sb("offset1", [P, BATCH])
        XT = sb("XT", [P, 2, GROUPS, TOK], F16)
        PHI = sb("PHI", [P, 4, E])
        RELU = sb("RELU", [P, 2, E])
        QT = [sb(f"QT{p}", [P, 2, GROUPS, TOK], F16) for p in range(2)]
        KT = sb("KT", [P, 2, GROUPS, TOK], F16)
        QS = [sb(f"QS{p}", [P, H, TOK], F16) for p in range(2)]
        KS = [sb(f"KS{p}", [P, H, TOK], F16) for p in range(2)]
        KN = [sb(f"KN{p}", [P, BATCH, 2, E], F16) for p in range(2)]
        VN = [sb(f"VN{p}", [P, BATCH, 2, H, DA], F16) for p in range(2)]
        AM = sb("AM", [P, 4, E])
        A = sb("A", [P, BATCH, 2, GROUPS, E], F16)
        wnat = [A[:, m].rearrange("p f g q -> p (f g q)").bitcast(F32).rearrange("p (c e) -> p c e", c=GROUPS)
                for m in range(2)]
        wnat += [QS[m][:].rearrange("p h t -> p (h t)").bitcast(F32).rearrange("p (c e) -> p c e", c=GROUPS)
                 for m in range(2)]
        DELTA = sb("DELTA", [P, 2, 2 * QUADS * DA])
        S = sb("S", [P, BATCH, 2, 2 * QUADS * DA])
        SH = sb("SH", [P, BATCH, 2, 2, 2 * QUADS * DA], F16)
        DEN = sb("DEN", [P, 2, H // 2])
        RDEN = sb("RDEN", [P, 2, H // 2])
        ATTN = sb("ATTN", [P, BATCH, E])
        AT = sb("AT", [P, BATCH, 2, E], F16)
        X2 = sb("X2", [P, BATCH, E])
        Y = sb("Y", [P, BATCH, E])
        raw2 = sb("raw2", [P, BATCH, 6])
        wsq = Y[:, 0]

        TP = [ps(f"TP{i}") for i in range(2)]
        PJ = [ps(f"PJ{i}") for i in range(2)]
        SC = [ps(f"SC{i}") for i in range(2)]
        AV = [ps(f"AV{i}") for i in range(2)]
        TP16 = [t[:].bitcast(F16) for t in TP]

        w_loaded = [sem(f"w_loaded{m}") for m in range(4)]
        norm_consts_loaded = sem("norm_consts_loaded")
        obias_loaded = sem("obias_loaded")
        consts_done = sem("consts_done")
        pool_step = sem("pool_step")
        w_summed = sem("w_summed")
        norm2_done = sem("norm2_done")
        norm2_reduced = sem("norm2_reduced")
        norm_done = sem("norm_done")
        scales_done = sem("scales_done")
        dve_setup = sem("dve_setup")
        wT_filled = sem("wT_filled")
        wT_hi = sem("wT_hi")
        wT_lo = sem("wT_lo")
        consts_scaled = sem("consts_scaled")
        zeroed = sem("zeroed")

        x_loaded = [sem(f"x_loaded{p}") for p in range(2)]
        stat0_raw, stat0_done = sig("stat0_raw", 2), sig("stat0_done", 2)
        stat1_raw, stat1_done = sig("stat1_raw", 2), sig("stat1_done", 2)
        stat2_raw, stat2_done = sig("stat2_raw", 2), sig("stat2_done", 2)
        var0_done, var1_done, var2_done = sig("var0_done", 1), sig("var1_done", 1), sig("var2_done", 1)
        neg_mean_done, offset1_done = sig("neg_mean_done", 1), sig("offset1_done", 1)
        rstd0_done, rstd1_done, rstd2_done = sig("rstd0_done", 1), sig("rstd1_done", 1), sig("rstd2_done", 1)
        xb_done, x1bo_done, x2b_done = sig("xb_done", 1), sig("x1bo_done", 1), sig("x2b_done", 1)
        x_gained, x1_done, xn_done = sig("x_gained", 2), sig("x1_done", 2), sig("xn_done", 2)
        xT_filled, xT_hi, xT_lo = sig("xT_filled", 2), sig("xT_hi", 2), sig("xT_lo", 2)
        q_filled, q_exp, q_relu = sig("q_filled", 2), sig("q_exp", 2), sig("q_relu", 2)
        q_phi, q_hi, q_lo = sig("q_phi", 2), sig("q_hi", 2), sig("q_lo", 2)
        k_filled, k_exp, k_relu = sig("k_filled", 2), sig("k_exp", 2), sig("k_relu", 2)
        k_phi, k_hi, k_lo = sig("k_phi", 2), sig("k_hi", 2), sig("k_lo", 2)
        v_filled, v_hi, v_lo = sig("v_filled", 2), sig("v_hi", 2), sig("v_lo", 2)
        kT_filled, kT_copied = sig("kT_filled", 2), sig("kT_copied", 2)
        q_stacked = [sem(f"q_stacked{p}") for p in range(2)]
        k_stacked = [sem(f"k_stacked{p}") for p in range(2)]
        sc_filled, sc_masked = sig("sc_filled", 8), sig("sc_masked", 4)
        sc_copied, sc_cut = sig("sc_copied", 4), sig("sc_cut", 4)
        a_hi, a_lo = sig("a_hi", 8), sig("a_lo", 8)
        av_filled, den_done, rden_done, attn_done = (sig("av_filled", 4), sig("den_done", 4),
                                                     sig("rden_done", 4), sig("attn_done", 4))
        st_filled, delta_done = sig("st_filled", 4), sig("delta_done", 4)
        s_added, s_hi, s_lo = sig("s_added", 4), sig("s_hi", 2), sig("s_lo", 2)
        attnT_filled, attnT_hi, attnT_lo = sig("attnT_filled", 2), sig("attnT_hi", 2), sig("attnT_lo", 2)
        out_filled, x2_done = sig("out_filled", 2), sig("x2_done", 2)
        x2_gained, y_done = sig("x2_gained", 2), sig("y_done", 2)
        y_stored = sig("y_stored", 1, 16)

        def par_at(i, by):
            if isinstance(i, int):
                return (i // 2 + 1) * by
            raise AssertionError

        steps = CHUNKS
        weights = (Wq, Wk, Wv, Wo)
        W_ORDER = (1, 0, 2, 3)
        PAIRS = ((1, 0), (2, 3))
        W_BANKS = PJ + (SC + AV) * 3 + SC
        W_REUSE = len(PJ + SC + AV)

        class Step:

            def __init__(self, t, r):
                self.t, self.r = t, r
                self.number = isinstance(t, int)

            def chunk(self, ahead):
                return self.t * 2 + (self.r + ahead)

            def parity(self, ahead):
                return (self.r + ahead) % 2

            def pair(self, ahead, by):
                return self.t * by + ((self.r + ahead) // 2 + 1) * by

            def has(self, ahead):
                return not self.number or 0 <= self.chunk(ahead) < steps

        def run_first(body):
            for s in (-3, -2):
                body(Step(0, s))

        def run(eng, body):
            for s in range(-1, 2):
                body(Step(0, s))
            with eng.Fori(1, steps // 2 - 2) as t:
                body(Step(t, 0))
                body(Step(t, 1))
            for s in range(steps - 4, steps + 1):
                body(Step(0, s))

        def pair_wait(eng, sems, st, ahead, by):
            eng.wait_ge(sems[st.parity(ahead)], st.pair(ahead, by))

        passed = {e: sem(f"passed_{e}") for e in ("sp", "pool", "dve")}

        def stand(eng, name):
            eng.sem_inc(passed[name], 1)

        block = ctx.enter_context(nc.Block())

        @block.sync
        def _(sp):
            def load_x(i):
                sp.dma_start(X[:, i], x[:, i * C:(i + 1) * C, :].rearrange("b p e -> p b e")).then_inc(x_loaded[i], 16)

            load_x(0)
            sp.dma_start(gain[:], ln_g.rearrange("(a n) -> a n", a=1).to_broadcast([P, E])).then_inc(norm_consts_loaded, 16)
            sp.dma_start(shift[:, 0], ln_b.rearrange("(a n) -> a n", a=1).to_broadcast([P, E])).then_inc(norm_consts_loaded, 16)
            for m in W_ORDER:
                sp.dma_start(wnat[m], weights[m].rearrange("(c p) e -> p c e", p=P)).then_inc(w_loaded[m], 16)
            for b in range(BATCH):
                sp.dma_start(obias[:, b], attn_bo.rearrange("(a n) -> a n", a=1).to_broadcast([P, E])).then_inc(obias_loaded, 16)
            load_x(1)

            def body(st):
                n, p = st.chunk(1), st.parity(1)
                if st.has(4) and (not st.number or st.chunk(4) >= 2):
                    wait(sp, x_gained, st.chunk(2), 1)
                    stand(sp, "sp")
                    wait(sp, xb_done, st.chunk(2))
                    stand(sp, "sp")
                    i = st.chunk(4)
                    start = i * C
                    sp.dma_start(X[:, st.parity(4)], x[:, bass.ds(start, C), :].rearrange("b p e -> p b e")).then_inc(x_loaded[st.parity(4)], 16)
                if st.has(1):
                    wait(sp, q_lo, n, 1)
                    if st.has(-1):
                        wait(sp, sc_filled, st.chunk(-1), 7)
                    for j, half in enumerate(Q_STACK):
                        for h in range(QUADS):
                            sp.dma_start(QS[p][D * j:D * j + D, h::QUADS, :],
                                         QT[p][D * h:D * h + D, half]).then_inc(q_stacked[p], 16)
                    wait(sp, kT_copied, n, 1)
                    for j, half in enumerate(K_STACK):
                        for h in range(QUADS):
                            sp.dma_start(KS[p][D * j:D * j + D, h::QUADS, :],
                                         KT[D * h:D * h + D, half]).then_inc(k_stacked[p], 16)
                if st.has(-1):
                    i = st.chunk(-1)
                    wait(sp, y_done, i, 1)
                    stand(sp, "sp")
                    sp.dma_start(out[:, bass.ds(i * C, C), :].rearrange("b p e -> p b e"), Y[:]).then_inc(y_stored.sem, 16)

            run_first(body)
            run(sp, body)
            wait(sp, y_stored, steps - 1)

        @block.gpsimd
        def _(pool):
            g = nc.gpsimd
            count = [0]

            def link(ins):
                count[0] += 1
                ins.then_inc(pool_step, 1)
                pool.wait_ge(pool_step, count[0])

            g.memset(neg_half[:], -0.5)
            g.memset(half4[:], 0.5)
            g.memset(minus_one[:], -1.0)
            g.memset(ident[:], 0.0)
            link(g.memset(causal[:], SUM_DOWN))
            g.memset(blocks[:], SUM_DOWN)
            link(g.affine_select(out=ident[:], in_=ident[:], compare_op=ALU.not_equal, fill=1.0, base=0,
                                 pattern=[[-1, P]], channel_multiplier=1))
            link(g.affine_select(out=causal[:], in_=causal[:], compare_op=ALU.is_ge, fill=0.0, base=0,
                                 pattern=[[1, P]], channel_multiplier=-1))
            link(g.affine_select(out=blocks[:], in_=blocks[:], compare_op=ALU.is_ge, fill=0.0, base=0,
                                 pattern=[[0, 2], [-D, QUADS], [0, DA]], channel_multiplier=1))
            link(g.affine_select(out=blocks[:], in_=blocks[:], compare_op=ALU.is_ge, fill=0.0, base=D - 1,
                                 pattern=[[0, 2], [D, QUADS], [0, DA]], channel_multiplier=-1))
            g.tensor_copy(ident16[:], ident[:]).then_inc(consts_done, 1)
            pool.wait_ge(consts_scaled, 3)
            pool.wait_ge(zeroed, 1)

            def rstd(var, var_done, rstd_, rstd_done, stat, stat_done, i, prev, double):
                if prev is not None:
                    wait(pool, rstd_done, prev)
                wait(pool, stat_done, i, 1)
                a, c = (1.0 + EPS, EPS * EPS) if double else (1.0, EPS)
                stand(pool, "pool")
                g.tensor_scalar(var[:], stat[:, :, 1], a, c, ALU.mult, ALU.add).then_inc(var_done.sem, 1)
                wait(pool, var_done, i)
                g.tensor_tensor(rstd_[:], var[:], neg_half[:], ALU.pow).then_inc(rstd_done.sem, 1)

            def norms(pair):
                at = slice(2 * pair, 2 * pair + 2)
                pool.wait_ge(norm2_done, pair + 1)
                g.partition_all_reduce(norm2_all[:, at], norm2[:, at], P, RMAX).then_inc(norm2_reduced, 1)
                pool.wait_ge(norm2_reduced, pair + 1)
                g.tensor_tensor(norm[:, at], norm2_all[:, at], half4[:, at], ALU.pow).then_inc(norm_done, 1)

            def body(st):
                s, n, f, back = st.chunk(0), st.chunk(1), st.chunk(2), st.chunk(-1)

                def x1_bias():
                    wait(pool, x1_done, n, 1)
                    if st.has(-1):
                        wait(pool, x2_done, back, 1)
                    g.tensor_tensor(X1BO[:, st.parity(1)], X1[:], obias[:], ALU.add).then_inc(x1bo_done.sem, 1)

                def x_shift():
                    pair_wait(pool, x_loaded, st, 3, 16)
                    if st.has(2):
                        wait(pool, x1_done, f, 1)
                    g.tensor_tensor(XB[:], X[:, st.parity(3)], shift[:], ALU.add).then_inc(xb_done.sem, 1)

                def x2_shift():
                    wait(pool, x2_gained, back, 1)
                    g.tensor_tensor(X2[:], X2[:], shift[:], ALU.add).then_inc(x2b_done.sem, 1)

                def norm_offset():
                    wait(pool, stat1_done, f, 1)
                    if st.has(1):
                        wait(pool, offset1_done, n)
                        wait(pool, xn_done, n, 1)
                    g.tensor_tensor(neg_mean[:], stat1[:, :, 0], minus_one[:], ALU.mult).then_inc(neg_mean_done.sem, 1)
                    wait(pool, neg_mean_done, f)
                    wait(pool, rstd1_done, f)
                    g.tensor_tensor(offset1[:], neg_mean[:], rstd1[:], ALU.mult).then_inc(offset1_done.sem, 1)

                def cut(b, hg):
                    k = b * GROUPS + hg
                    wait(pool, sc_copied, s, k // 2)
                    stand(pool, "pool")
                    am = AM[:, k % 4].rearrange("p (h q) -> p h q", h=QUADS)
                    g.affine_select(out=am, in_=am, compare_op=ALU.is_ge, fill=0.0, base=0,
                                    pattern=[[0, QUADS], [1, C]], channel_multiplier=-1).then_inc(sc_cut.sem, 1)

                def split_a(b, hg):
                    k = b * GROUPS + hg
                    wait(pool, a_hi, s, k)
                    g.tensor_tensor(A[:, b, LO, hg], AM[:, k % 4], A[:, b, HI, hg], ALU.subtract).then_inc(a_lo.sem, 1)

                def add_s(b, hf):
                    wait(pool, delta_done, s, 2 * b + hf)
                    if hf == 0 and st.has(-1):
                        wait(pool, s_hi, back, b)
                        wait(pool, s_lo, back, b)
                    g.tensor_tensor(S[:, b, hf], S[:, b, hf], DELTA[:, hf], ALU.add).then_inc(s_added.sem, 1)

                def split_s(b):
                    wait(pool, s_hi, s, b)
                    g.tensor_tensor(SH[:, b, LO], S[:, b], SH[:, b, HI], ALU.subtract).then_inc(s_lo.sem, 1)

                A_, B_, F_, K_ = st.has(1), st.has(0), st.has(2), st.has(-1)
                if K_:
                    rstd(var2, var2_done, rstd2, rstd2_done, stat2, stat2_done, back,
                         st.chunk(-2) if st.has(-2) else None, True)
                if A_:
                    if not B_:
                        pool.wait_ge(obias_loaded, 16 * BATCH)
                    x1_bias()
                if F_:
                    if A_:
                        wait(pool, x1_done, n, 1)
                    rstd(var0, var0_done, rstd0, rstd0_done, stat0, stat0_done, f, n if A_ else None, True)
                    if not A_:
                        norms(0)
                if B_:
                    cut(0, 1)
                    split_a(0, 0)
                    split_a(0, 1)
                    cut(0, 3)
                    split_a(0, 2)
                    split_a(0, 3)
                if F_:
                    if A_:
                        wait(pool, xn_done, n, 1)
                    rstd(var1, var1_done, rstd1, rstd1_done, stat1, stat1_done, f, n if A_ else None, False)
                    norm_offset()
                    if not A_:
                        norms(1)
                if B_:
                    cut(1, 1)
                    split_a(1, 0)
                    split_a(1, 1)
                    cut(1, 3)
                    split_a(1, 2)
                    split_a(1, 3)
                    add_s(0, 0)
                    add_s(0, 1)
                if K_:
                    x2_shift()
                if B_:
                    add_s(1, 0)
                    add_s(1, 1)
                if st.has(3):
                    x_shift()
                if B_:
                    split_s(0)
                    split_s(1)

            run_first(body)
            run(pool, body)

        @block.scalar
        def _(act):
            a = nc.scalar

            def square(j):
                m = W_ORDER[j]
                act.wait_ge(w_loaded[m], 16)
                for c in range(GROUPS):
                    a.activation(wsq, wnat[m][:, c], ACT.Square, accum_out=sumsq[:, m, c:c + 1]).then_inc(w_summed, 1)
                    act.wait_ge(w_summed, j * GROUPS + c + 1)

            def w_half(j):
                m = W_ORDER[j]
                act.wait_ge(scales_done, j // 2 + 1)
                for c in range(GROUPS):
                    k = j * GROUPS + c
                    act.wait_ge(wT_filled, k + 1)
                    a.activation(wT[m][:, HI, c], W_BANKS[k][:], ACT.Copy, scale=w_scale[:, m:m + 1]).then_inc(wT_hi, 1)

            square(0)
            square(1)

            def body(st):
                s, n, f, back = st.chunk(0), st.chunk(1), st.chunk(2), st.chunk(-1)
                A_, B_, F_, K_ = st.has(1), st.has(0), st.has(2), st.has(-1)

                def normalise(b):
                    wait(act, offset1_done, f)
                    if A_ and b == 0:
                        wait(act, xT_filled, n, 1)
                    a.activation(XN[:, b], X1[:, b], ACT.Identity, bias=offset1[:, b:b + 1],
                                 scale=rstd1[:, b:b + 1]).then_inc(xn_done.sem, 1)

                def x_half(b):
                    wait(act, xT_filled, f, b)
                    if A_:
                        wait(act, v_filled, n, 1)
                    a.activation(XT[:, HI, :, b * C:(b + 1) * C], TP[b][:].rearrange("p (c t) -> p c t", c=GROUPS),
                                 ACT.Copy, scale=X_UP).then_inc(xT_hi.sem, 1)

                def exp_relu_k(b):
                    wait(act, k_filled, n, b)
                    if B_:
                        wait(act, k_lo, s, b)
                        wait(act, q_phi, s, b)
                    a.activation(PHI[:, b], PJ[b][:], ACT.Exp, scale=inv_scale[:, 1:2]).then_inc(k_exp.sem, 1)
                    a.activation(RELU[:, b], PJ[b][:], ACT.Relu, scale=inv_scale[:, 1:2]).then_inc(k_relu.sem, 1)

                def exp_relu_q(pr):
                    wait(act, q_filled, n, pr)
                    if B_:
                        wait(act, q_lo, s, pr)
                    wait(act, k_phi, n, pr)
                    a.activation(PHI[:, 2 + pr], PJ[pr][:], ACT.Exp, scale=inv_scale[:, 0:1]).then_inc(q_exp.sem, 1)
                    a.activation(RELU[:, pr], PJ[pr][:], ACT.Relu, scale=inv_scale[:, 0:1]).then_inc(q_relu.sem, 1)

                def q_half(pr):
                    wait(act, q_phi, n, pr)
                    if K_ and pr == 0:
                        wait(act, av_filled, back, 3)
                        pair_wait(act, q_stacked, st, -1, 16 * RESTACKS)
                    a.activation(QT[st.parity(1)][:, HI, 2 * pr:2 * pr + 2], PHI[:, 2 + pr].rearrange("p (g t) -> p g t", g=2),
                                 ACT.Copy, scale=f_scale[:, 0:1]).then_inc(q_hi.sem, 1)

                def k_half(b):
                    wait(act, k_phi, n, b)
                    if K_:
                        wait(act, st_filled, back, 2 * b + 1)
                    a.activation(KN[st.parity(1)][:, b, HI], PHI[:, b], ACT.Copy, scale=f_scale[:, 1:2]).then_inc(k_hi.sem, 1)

                def copy_scores(b, hg):
                    k = b * GROUPS + hg
                    wait(act, sc_filled, s, k)
                    if k >= 4:
                        wait(act, a_lo, s, k - 4)
                    elif K_:
                        wait(act, a_lo, back, k + 4)
                    a.activation(AM[:, k % 4], SC[hg % 2][:], ACT.Copy, scale=SUM_DOWN).then_inc(sc_copied.sem, 1)

                def split_a(b, hg):
                    k = b * GROUPS + hg
                    wait(act, sc_cut if hg % 2 else sc_masked, s, k // 2)
                    if hg == 0 and K_:
                        wait(act, av_filled, back, 2 * b + 1)
                    a.activation(A[:, b, HI, hg], AM[:, k % 4], ACT.Copy).then_inc(a_hi.sem, 1)

                def kT(b):
                    wait(act, kT_filled, n, b)
                    if B_ and b == 0:
                        pair_wait(act, k_stacked, st, 0, 16 * RESTACKS)
                    a.activation(KT[:, :, :, b * C:(b + 1) * C],
                                 TP16[b].rearrange("p (f c t) -> p f c t", f=2, c=GROUPS),
                                 ACT.Copy).then_inc(kT_copied.sem, 1)

                def v_half(b):
                    wait(act, v_filled, n, b)
                    if K_:
                        wait(act, st_filled, back, 2 * b + 1)
                    a.activation(VN[st.parity(1)][:, b, HI, :, 0:D], PJ[b][:].rearrange("p (h d) -> p h d", h=H),
                                 ACT.Copy, scale=V_SCALE).then_inc(v_hi.sem, 1)

                def attn_half(b):
                    wait(act, attnT_filled, s, b)
                    if K_:
                        wait(act, out_filled, back, b)
                    a.activation(AT[:, b, HI], TP[b][:], ACT.Copy, scale=ATTN_UP).then_inc(attnT_hi.sem, 1)

                def s_half(b):
                    wait(act, s_added, s, 2 * b + 1)
                    wait(act, av_filled, s, 2 * b + 1)
                    a.activation(SH[:, b, HI], S[:, b], ACT.Copy).then_inc(s_hi.sem, 1)

                if F_ and not A_:
                    normalise(0)
                    normalise(1)
                    w_half(0)
                    x_half(0)
                    x_half(1)
                    square(2)
                    square(3)
                    w_half(1)
                    return
                if A_:
                    exp_relu_k(0)
                    exp_relu_k(1)
                    if not B_:
                        w_half(2)
                    if not K_:
                        k_half(0)
                        k_half(1)
                if B_:
                    copy_scores(0, 1)
                    split_a(0, 0)
                if A_ and K_:
                    k_half(0)
                    k_half(1)
                if B_:
                    split_a(0, 1)
                    copy_scores(0, 3)
                if A_:
                    exp_relu_q(0)
                if B_:
                    split_a(0, 2)
                    split_a(0, 3)
                if A_:
                    exp_relu_q(1)
                    q_half(0)
                    kT(0)
                if B_:
                    copy_scores(1, 1)
                    split_a(1, 0)
                    split_a(1, 1)
                if A_:
                    q_half(1)
                    if not B_:
                        normalise(0)
                        normalise(1)
                    kT(1)
                    v_half(0)
                if B_:
                    copy_scores(1, 3)
                    split_a(1, 2)
                    split_a(1, 3)
                if A_:
                    v_half(1)
                if F_ and B_:
                    normalise(0)
                    normalise(1)
                if B_:
                    attn_half(0)
                    attn_half(1)
                if F_:
                    x_half(0)
                if B_:
                    s_half(0)
                    s_half(1)
                if F_:
                    x_half(1)
                if A_ and not B_:
                    w_half(3)

            run_first(body)
            run(act, body)

        @block.vector
        def _(dve):
            v = nc.vector
            count = [0]

            def link(ins):
                count[0] += 1
                ins.then_inc(dve_setup, 1)
                dve.wait_ge(dve_setup, count[0])

            link(v.memset(S[:], 0.0))
            link(v.memset(SH[:], 0.0))
            for p in range(2):
                link(v.memset(VN[p][:, :, HI, :, D:DA], ATTN_UP))
                link(v.memset(VN[p][:, :, LO, :, D:DA], 0.0))
            dve.wait_ge(norm_consts_loaded, 16 * 2)
            v.tensor_scalar(shift[:, 1], shift[:, 0], 0.5, None, ALU.mult).then_inc(consts_scaled, 1)
            v.tensor_scalar(gain[:], gain[:], 0.5, None, ALU.mult).then_inc(consts_scaled, 1)
            dve.wait_ge(consts_scaled, 1)
            v.tensor_copy(shift[:, 0], shift[:, 1]).then_inc(consts_scaled, 1)
            dve.wait_ge(consts_scaled, 3)
            v.memset(DEN[:], 1.0).then_inc(zeroed, 1)
            dve.wait_ge(zeroed, 1)
            dve.wait_ge(consts_done, 1)

            def row_sums(pair):
                at = slice(2 * pair, 2 * pair + 2)
                dve.wait_ge(w_summed, (pair + 1) * 2 * GROUPS)
                link(v.tensor_reduce(norm2[:, at], sumsq[:, at], mybir.AxisListType.X, ALU.max))
                v.tensor_scalar(norm2[:, at], norm2[:, at], 1e-30, None, ALU.max).then_inc(norm2_done, 1)

            def scales(pair):
                at = slice(2 * pair, 2 * pair + 2)
                dve.wait_ge(norm_done, pair + 1)
                link(v.tensor_scalar(pow2[:, at].bitcast(U32), norm[:, at].bitcast(U32), 0x7F800000, None, ALU.bitwise_and))
                link(v.reciprocal(rpow2[:, at], pow2[:, at]))
                link(v.tensor_scalar(w_scale[:, at], rpow2[:, at], TOP, None, ALU.mult))
                if pair == 0:
                    link(v.tensor_scalar(inv_scale[:], pow2[:, at], 1.0 / (TOP * X_UP), None, ALU.mult))
                    link(v.tensor_scalar(f_bound[:], pow2[:, at], 64.0, 1.0, ALU.mult, ALU.max))
                    link(v.reciprocal(f_scale[:], f_bound[:]))
                    link(v.tensor_scalar(f_scale[:], f_scale[:], TOP, None, ALU.mult))
                    link(v.tensor_tensor(den_eps[:], f_scale[:, 0:1], f_scale[:, 1:2], ALU.mult))
                    v.tensor_scalar(den_eps[:], den_eps[:], SUM_DOWN * ATTN_UP, EPS, ALU.mult, ALU.mult).then_inc(scales_done, 1)
                else:
                    link(v.tensor_tensor(out_scale[:], pow2[:, 2:3], pow2[:, 3:4], ALU.mult))
                    v.tensor_scalar(out_scale[:], out_scale[:], 1.0 / (TOP * X_UP * V_SCALE * TOP), None, ALU.mult).then_inc(scales_done, 1)
                dve.wait_ge(scales_done, pair + 1)

            def w_low(j):
                m = W_ORDER[j]
                for c in range(GROUPS):
                    k = j * GROUPS + c
                    dve.wait_ge(wT_hi, k + 1)
                    v.scalar_tensor_tensor(wT[m][:, LO, c], W_BANKS[k][:], w_scale[:, m:m + 1], wT[m][:, HI, c],
                                           ALU.mult, ALU.subtract).then_inc(wT_lo, 1)

            def stats(src, rawt, stat, raw_sig, done_sig, i, b):
                v.bn_stats(rawt[:, b], src).then_inc(raw_sig.sem, 1)
                wait(dve, raw_sig, i, b)
                stand(dve, "dve")
                v.bn_aggr(stat[:, b], rawt[:, b]).then_inc(done_sig.sem, 1)

            def body(st):
                s, n, f, back = st.chunk(0), st.chunk(1), st.chunk(2), st.chunk(-1)
                A_, B_, F_, K_ = st.has(1), st.has(0), st.has(2), st.has(-1)

                def front_stats(b):
                    if b == 0:
                        pair_wait(dve, x_loaded, st, 2, 16)
                        if st.has(1):
                            wait(dve, var0_done, n)
                            wait(dve, x_gained, n, 1)
                            wait(dve, stat1_done, n, 1)
                    stats(X[:, st.parity(2), b], raw, stat0, stat0_raw, stat0_done, f, b)

                def front_gain(b):
                    if st.has(-2):
                        wait(dve, y_done, st.chunk(-2), b)
                    elif A_:
                        wait(dve, x1_done, n, b)
                    v.scalar_tensor_tensor(GAINED[:, b], X[:, st.parity(2), b], stat0[:, b, 0:1], gain[:],
                                           ALU.subtract, ALU.mult).then_inc(x_gained.sem, 1)

                def front_x1(b):
                    wait(dve, x_gained, f, b)
                    if b == 0:
                        wait(dve, rstd0_done, f)
                        wait(dve, xb_done, f)
                        if st.has(1):
                            wait(dve, x1bo_done, n)
                            wait(dve, xn_done, n, 1)
                    v.scalar_tensor_tensor(X1[:, b], GAINED[:, b], rstd0[:, b:b + 1], XB[:, b],
                                           ALU.mult, ALU.add).then_inc(x1_done.sem, 1)

                def front_stats1(b):
                    wait(dve, x1_done, f, b)
                    if b == 0 and st.has(1):
                        wait(dve, var1_done, n)
                    stats(X1[:, b], raw, stat1, stat1_raw, stat1_done, f, b)

                def x_low(b):
                    wait(dve, xT_hi, f, b)
                    v.scalar_tensor_tensor(XT[:, LO, :, b * C:(b + 1) * C],
                                           TP[b][:].rearrange("p (c t) -> p c t", c=GROUPS), X_UP,
                                           XT[:, HI, :, b * C:(b + 1) * C],
                                           ALU.mult, ALU.subtract).then_inc(xT_lo.sem, 1)

                def mask(b, hg):
                    assert hg % 2 == 0
                    k = b * GROUPS + hg
                    wait(dve, sc_filled, s, k)
                    if k >= 4:
                        wait(dve, a_lo, s, k - 4)
                    elif K_:
                        wait(dve, a_lo, back, k + 4)
                    v.tensor_tensor(AM[:, k % 4].rearrange("p (h q) -> p h q", h=QUADS),
                                    SC[hg % 2][:].rearrange("p (h q) -> p h q", h=QUADS),
                                    causal[:].unsqueeze(1).to_broadcast([P, QUADS, C]),
                                    ALU.mult).then_inc(sc_masked.sem, 1)

                def phi_q(pr):
                    wait(dve, q_relu, n, pr)
                    v.scalar_tensor_tensor(PHI[:, 2 + pr], PHI[:, 2 + pr], 1.0, RELU[:, pr],
                                           ALU.min, ALU.add).then_inc(q_phi.sem, 1)

                def low_q(pr):
                    wait(dve, q_hi, n, pr)
                    v.scalar_tensor_tensor(QT[st.parity(1)][:, LO, 2 * pr:2 * pr + 2],
                                           PHI[:, 2 + pr].rearrange("p (g t) -> p g t", g=2), f_scale[:, 0:1],
                                           QT[st.parity(1)][:, HI, 2 * pr:2 * pr + 2],
                                           ALU.mult, ALU.subtract).then_inc(q_lo.sem, 1)

                def phi_k(b):
                    wait(dve, k_relu, n, b)
                    v.scalar_tensor_tensor(PHI[:, b], PHI[:, b], 1.0, RELU[:, b],
                                           ALU.min, ALU.add).then_inc(k_phi.sem, 1)

                def low_k(b):
                    wait(dve, k_hi, n, b)
                    v.scalar_tensor_tensor(KN[st.parity(1)][:, b, LO], PHI[:, b], f_scale[:, 1:2],
                                           KN[st.parity(1)][:, b, HI], ALU.mult, ALU.subtract).then_inc(k_lo.sem, 1)

                def low_v(b):
                    wait(dve, v_hi, n, b)
                    v.scalar_tensor_tensor(VN[st.parity(1)][:, b, LO, :, 0:D], PJ[b][:].rearrange("p (h d) -> p h d", h=H),
                                           V_SCALE, VN[st.parity(1)][:, b, HI, :, 0:D],
                                           ALU.mult, ALU.subtract).then_inc(v_lo.sem, 1)

                def quotient(b, hf):
                    k = 2 * b + hf
                    wait(dve, av_filled, s, k)
                    av = AV[hf][:, 0:2 * QUADS * DA].rearrange("p (h d) -> p h d", d=DA)
                    if b == 1:
                        wait(dve, attn_done, s, hf)
                    elif K_:
                        wait(dve, attn_done, back, 2 + hf)
                    v.tensor_scalar(DEN[:, hf], av[:, :, D], den_eps[:], None, ALU.add).then_inc(den_done.sem, 1)
                    wait(dve, den_done, s, k)
                    v.reciprocal(RDEN[:, hf], DEN[:, hf]).then_inc(rden_done.sem, 1)
                    wait(dve, rden_done, s, k)
                    if K_ and hf == 0:
                        wait(dve, attnT_filled, back, b)
                    v.tensor_tensor(ATTN[:, b, hf * (E // 2):(hf + 1) * (E // 2)].rearrange("p (h d) -> p h d", d=D),
                                    av[:, :, 0:D], RDEN[:, hf].unsqueeze(2).to_broadcast([P, H // 2, D]),
                                    ALU.mult).then_inc(attn_done.sem, 1)

                def delta(b, hf):
                    k = 2 * b + hf
                    wait(dve, st_filled, s, k)
                    if b == 1:
                        wait(dve, s_added, s, hf)
                    elif K_:
                        wait(dve, s_added, back, 2 + hf)
                    v.tensor_tensor(DELTA[:, hf], PJ[hf][:, 0:2 * QUADS * DA],
                                    blocks[:].rearrange("p g h d -> p (g h d)"), ALU.mult).then_inc(delta_done.sem, 1)

                def attn_low(b):
                    wait(dve, attnT_hi, s, b)
                    v.scalar_tensor_tensor(AT[:, b, LO], TP[b][:], ATTN_UP, AT[:, b, HI],
                                           ALU.mult, ALU.subtract).then_inc(attnT_lo.sem, 1)

                def add_out(b):
                    wait(dve, out_filled, s, b)
                    if b == 0:
                        wait(dve, x1bo_done, s)
                        if K_:
                            wait(dve, y_done, back, 1)
                            wait(dve, var2_done, back)
                    v.scalar_tensor_tensor(X2[:, b], PJ[b][:], out_scale[:], X1BO[:, st.parity(0), b],
                                           ALU.mult, ALU.add).then_inc(x2_done.sem, 1)
                    wait(dve, x2_done, s, b)
                    stats(X2[:, b], raw2, stat2, stat2_raw, stat2_done, s, b)

                def back_gain(b):
                    if F_:
                        wait(dve, x1_done, f, b)
                    elif A_:
                        wait(dve, x1_done, n, b)
                    wait(dve, stat2_done, back, b)
                    v.scalar_tensor_tensor(GAINED[:, b], X2[:, b], stat2[:, b, 0:1], gain[:],
                                           ALU.subtract, ALU.mult).then_inc(x2_gained.sem, 1)

                def back_y(b):
                    wait(dve, x2_gained, back, b)
                    if b == 0:
                        wait(dve, rstd2_done, back)
                        wait(dve, x2b_done, back)
                        if st.has(-2):
                            wait(dve, y_stored, st.chunk(-2))
                    v.scalar_tensor_tensor(Y[:, b], GAINED[:, b], rstd2[:, b:b + 1], X2[:, b],
                                           ALU.mult, ALU.add).then_inc(y_done.sem, 1)

                def both(on, fn, *args):
                    if on:
                        for b in range(BATCH):
                            fn(b, *args)

                both(F_, front_stats)
                if F_:
                    wait(dve, stat0_done, f, 1)
                both(F_, front_gain)
                if F_ and not A_:
                    both(True, front_x1)
                    both(True, front_stats1)
                    row_sums(0)
                    scales(0)
                    w_low(0)
                    both(True, x_low)
                    row_sums(1)
                    w_low(1)
                    scales(1)
                    return
                if A_:
                    phi_k(0)
                if A_ and not K_:
                    phi_k(1)
                    low_k(0)
                    low_k(1)
                if A_ and not B_:
                    w_low(2)
                if B_:
                    mask(0, 0)
                if A_ and K_:
                    phi_k(1)
                both(F_, front_x1)
                if A_ and K_:
                    low_k(0)
                if B_:
                    mask(0, 2)
                if A_ and K_:
                    low_k(1)
                if A_:
                    phi_q(0)
                both(F_, front_stats1)
                if A_:
                    phi_q(1)
                    low_q(0)
                if B_:
                    mask(1, 0)
                    quotient(0, 0)
                both(K_, back_gain)
                if A_:
                    low_q(1)
                if B_:
                    mask(1, 2)
                if A_:
                    low_v(0)
                if B_:
                    quotient(0, 1)
                if A_:
                    low_v(1)
                if B_:
                    quotient(1, 0)
                    delta(0, 0)
                    delta(0, 1)
                    quotient(1, 1)
                    attn_low(0)
                    delta(1, 0)
                    delta(1, 1)
                    attn_low(1)
                if F_:
                    x_low(0)
                both(K_, back_y)
                if B_:
                    add_out(0)
                    add_out(1)
                if F_:
                    x_low(1)
                if A_ and not B_:
                    w_low(3)

            run_first(body)
            run(dve, body)

        @block.tensor
        def _(pe):
            t_ = nc.tensor
            pe.wait_ge(consts_done, 1)
            pe.wait_ge(zeroed, 1)

            def w_transposes(first, last):
                for k in range(first, last):
                    m, c = W_ORDER[k // GROUPS], k % GROUPS
                    pe.wait_ge(w_loaded[m], 16)
                    if k >= W_REUSE:
                        pe.wait_ge(wT_lo, k - len(SC + AV) + 1)
                    for o in range(GROUPS):
                        ins = t_.transpose(W_BANKS[k][:, o * P:(o + 1) * P],
                                           wnat[m][:, o, c * P:(c + 1) * P], ident[:])
                    ins.then_inc(wT_filled, 1)

            def body(st):
                s, n, f, back = st.chunk(0), st.chunk(1), st.chunk(2), st.chunk(-1)
                A_, B_, F_, K_ = st.has(1), st.has(0), st.has(2), st.has(-1)
                cur, nxt = st.parity(0), st.parity(1)

                def x_transposes(b):
                    wait(pe, xn_done, f, b)
                    if B_:
                        wait(pe, attnT_lo, s, b)
                    elif A_:
                        wait(pe, kT_copied, n, b)
                    for c in range(GROUPS):
                        ins = t_.transpose(TP[b][:, c * P:(c + 1) * P], XN[:, b, c * P:(c + 1) * P], ident[:])
                    ins.then_inc(xT_filled.sem, 1)

                def bank_free(b):
                    if K_:
                        wait(pe, x2_done, back, b)
                    elif B_:
                        wait(pe, v_lo, s, b)

                def project_q(pr):
                    wait(pe, k_relu, n, pr)
                    for g in range(2):
                        fb = 2 * pr + g
                        todo = [(c, w, m) for c in range(GROUPS) for w, m in PASSES]
                        for c, w, m in todo:
                            ins = t_.matmul(PJ[pr][:, g * TOK:(g + 1) * TOK], wT[0][:, w, c, fb * P:(fb + 1) * P],
                                            XT[:, m, c, :], start=(c, w, m) == todo[0], stop=(c, w, m) == todo[-1])
                    ins.then_inc(q_filled.sem, 1)

                def project(m_, b, filled):
                    todo = [(c, w, m) for c in range(GROUPS) for w, m in PASSES]
                    for c, w, m in todo:
                        ins = t_.matmul(PJ[b][:], XT[:, w, c, b * C:(b + 1) * C], wT[m_][:, m, c, :],
                                        start=(c, w, m) == todo[0], stop=(c, w, m) == todo[-1])
                    ins.then_inc(filled.sem, 1)

                def k_transposes(b):
                    wait(pe, k_lo, n, b)
                    wait(pe, xT_lo, n, b)
                    for half in (HI, LO):
                        for c in range(GROUPS):
                            at = (half * GROUPS + c) * P
                            ins = t_.transpose(TP16[b][:, at:at + P], KN[nxt][:, b, half, c * P:(c + 1) * P], ident16[:])
                    ins.then_inc(kT_filled.sem, 1)

                def scores(b, hg):
                    k = b * GROUPS + hg
                    if k == 0:
                        pair_wait(pe, q_stacked, st, 0, 16 * RESTACKS)
                        pair_wait(pe, k_stacked, st, 0, 16 * RESTACKS)
                    reader = sc_copied if hg % 2 else sc_masked
                    if k >= 2:
                        wait(pe, reader, s, k // 2 - 1)
                    elif K_:
                        wait(pe, reader, back, 3)
                    for h in range(QUADS):
                        head = hg * QUADS + h
                        ins = t_.matmul(SC[hg % 2][:, h * C:(h + 1) * C], KS[cur][0:STACK, head, b * C:(b + 1) * C],
                                        QS[cur][0:STACK, head, b * C:(b + 1) * C], start=True, stop=True)
                    ins.then_inc(sc_filled.sem, 1)

                def attend(b, hf):
                    wait(pe, a_lo, s, b * GROUPS + 2 * hf + 1)
                    if K_ and hf == 0:
                        wait(pe, s_lo, back, b)
                    if b == 1:
                        wait(pe, attn_done, s, hf)
                    elif K_:
                        wait(pe, attn_done, back, 2 + hf)
                    for g in range(2):
                        hg = 2 * hf + g
                        w_ = QUADS * DA
                        for w, m in PASSES:
                            t_.matmul(AV[hf][:, g * w_:(g + 1) * w_], QT[cur][:, w, hg, b * C:(b + 1) * C],
                                      SH[:, b, m, hf, g * w_:(g + 1) * w_], start=(w, m) == PASSES[0], stop=False)
                        for h in range(QUADS):
                            for w, m in PASSES:
                                ins = t_.matmul(AV[hf][:, g * w_ + h * DA:g * w_ + (h + 1) * DA],
                                                A[:, b, w, hg, h * C:(h + 1) * C], VN[cur][:, b, m, hg * QUADS + h, :],
                                                start=False, stop=(h == QUADS - 1 and (w, m) == PASSES[-1]))
                    ins.then_inc(av_filled.sem, 1)

                def update(b, hf):
                    w_ = QUADS * DA
                    for g in range(2):
                        hg = 2 * hf + g
                        for w, m in PASSES:
                            ins = t_.matmul(PJ[hf][:, g * w_:(g + 1) * w_], KN[cur][:, b, w, hg * P:(hg + 1) * P],
                                            VN[cur][:, b, m, hg * QUADS:(hg + 1) * QUADS, :],
                                            start=(w, m) == PASSES[0], stop=(w, m) == PASSES[-1])
                    ins.then_inc(st_filled.sem, 1)

                def attn_transposes(b):
                    wait(pe, attn_done, s, 2 * b + 1)
                    if A_:
                        wait(pe, kT_copied, n, b)
                    else:
                        wait(pe, attnT_lo, back, b)
                    for c in range(GROUPS):
                        ins = t_.transpose(TP[b][:, c * P:(c + 1) * P], ATTN[:, b, c * P:(c + 1) * P], ident[:])
                    ins.then_inc(attnT_filled.sem, 1)

                def project_out(b):
                    wait(pe, attnT_lo, s, b)
                    wait(pe, delta_done, s, 2 + b)
                    todo = [(c, w, m) for c in range(GROUPS) for w, m in PASSES]
                    for c, w, m in todo:
                        ins = t_.matmul(PJ[b][:], AT[:, b, w, c * C:(c + 1) * C], wT[3][:, m, c, :],
                                        start=(c, w, m) == todo[0], stop=(c, w, m) == todo[-1])
                    ins.then_inc(out_filled.sem, 1)

                if F_ and not A_:
                    w_transposes(0, W_REUSE)
                    x_transposes(0)
                    x_transposes(1)
                    w_transposes(W_REUSE, 2 * GROUPS)
                    return
                if A_:
                    if not B_:
                        pe.wait_ge(wT_lo, GROUPS)
                    wait(pe, xT_lo, n, 0)
                    bank_free(0)
                    project(1, 0, k_filled)
                    wait(pe, xT_lo, n, 1)
                    bank_free(1)
                    project(1, 1, k_filled)
                if A_ and not B_:
                    w_transposes(2 * GROUPS, 3 * GROUPS)
                    pe.wait_ge(wT_lo, 2 * GROUPS)
                if B_ and K_:
                    scores(0, 0)
                    scores(0, 1)
                if A_:
                    project_q(0)
                if B_ and not K_:
                    project_q(1)
                    pe.wait_ge(wT_lo, 4 * GROUPS)
                    scores(0, 0)
                    scores(0, 1)
                if B_:
                    scores(0, 2)
                    scores(0, 3)
                if A_:
                    if not B_ or K_:
                        project_q(1)
                    k_transposes(0)
                    k_transposes(1)
                    if not B_:
                        w_transposes(3 * GROUPS, 4 * GROUPS)
                if B_:
                    scores(1, 0)
                    scores(1, 1)
                    attend(0, 0)
                if A_ and not B_:
                    pe.wait_ge(wT_lo, 3 * GROUPS)
                if A_:
                    wait(pe, q_relu, n, 0)
                    project(2, 0, v_filled)
                if B_:
                    scores(1, 2)
                    scores(1, 3)
                    attend(0, 1)
                if A_:
                    wait(pe, q_relu, n, 1)
                    project(2, 1, v_filled)
                if B_:
                    if A_:
                        wait(pe, v_lo, n, 0)
                    else:
                        wait(pe, x2_done, back, 0)
                    update(0, 0)
                    attend(1, 0)
                    if A_:
                        wait(pe, v_lo, n, 1)
                    else:
                        wait(pe, x2_done, back, 1)
                    update(0, 1)
                    attend(1, 1)
                    attn_transposes(0)
                    wait(pe, delta_done, s, 0)
                    update(1, 0)
                    wait(pe, delta_done, s, 1)
                    update(1, 1)
                    attn_transposes(1)
                if F_:
                    x_transposes(0)
                if B_:
                    project_out(0)
                    project_out(1)
                if F_:
                    x_transposes(1)

            run_first(body)
            run(pe, body)


_INS = ['L0_attn_x', 'L0_attn_Wq', 'L0_attn_Wk', 'L0_attn_Wv', 'L0_attn_Wo', 'L0_attn_bo', 'L0_ffn_ln_g', 'L0_ffn_ln_b']
_OUTS = [((BATCH, LEN, E), 'float32')]


def kernel(**inputs):
    import numpy as _np
    import concourse.bacc as _bacc
    from concourse import mybir as _mybir
    from concourse.bass_utils import run_bass_kernel_spmd as _run

    nc = _bacc.Bacc("TRN2", target_bir_lowering=False, num_devices=1)
    arrays, args = {}, []
    for name in _INS:
        a = _np.ascontiguousarray(inputs[name])
        arrays[f"in_{name}_dram"] = a
        args.append(nc.dram_tensor(f"in_{name}_dram", a.shape, _mybir.dt.from_np(a.dtype), kind="ExternalInput").ap())
    for i, (shape, dtype) in enumerate(_OUTS):
        dt = _mybir.dt.from_np(_np.dtype(dtype))
        args.append(nc.dram_tensor(f"out_{i}_dram", shape, dt, kind="ExternalOutput").ap())
    build(nc, *args)
    r = _run(nc, [arrays], core_ids=[0])
    got = tuple(r.results[0][f"out_{i}_dram"] for i in range(len(_OUTS)))
    return got[0]
```

```python
from contextlib import ExitStack

import concourse.bass as bass
from concourse import mybir

P = 128
BATCH, LEN, E = 2, 4096, 512
H, D = 16, 32
QUADS = P // D
GROUPS = E // P
C = 128
CHUNKS = LEN // C
DA = D + 1
TOK = BATCH * C
EPS = 1e-5

X_UP = 64.0
TOP = 2.0 ** 14
SUM_DOWN = 2.0 ** -27
V_SCALE = 2.0 ** -11
ATTN_UP = 2.0 ** 15

F32 = mybir.dt.float32
F16 = mybir.dt.float16
U32 = mybir.dt.uint32
ALU = mybir.AluOpType
ACT = mybir.ActivationFunctionType
RMAX = bass.bass_isa.ReduceOp.max

HI, LO = 0, 1
PASSES = ((HI, HI), (HI, LO), (LO, HI))
K_STACK = (HI, HI, LO)
Q_STACK = (HI, LO, HI)
STACK = len(K_STACK) * D
RESTACKS = QUADS * len(K_STACK)


class Signal:

    def __init__(self, sem, per, by=1, base=0):
        self.sem, self.per, self.by, self.base = sem, per, by, base

    def at(self, i, k=0):
        return i * (self.per * self.by) + (self.base + self.by * (k + 1))


def wait(eng, signal, i, k=0):
    if isinstance(i, int) and i < 0:
        return
    eng.wait_ge(signal.sem, signal.at(i, k))


def build(nc, x, Wq, Wk, Wv, Wo, attn_bo, ln_g, ln_b, out):
    with ExitStack() as ctx:
        def sb(name, shape, dt=F32):
            return ctx.enter_context(nc.sbuf_tensor(name, shape, dt))

        def ps(name, shape=(P, E), dt=F32):
            return ctx.enter_context(nc.psum_tensor(name, list(shape), dt))

        def sem(name):
            return ctx.enter_context(nc.semaphore(name))

        def sig(name, per, by=1, base=0):
            return Signal(sem(name), per, by, base)

        ident = sb("ident", [P, P])
        ident16 = sb("ident16", [P, P], F16)
        causal = sb("causal", [P, P])
        blocks = sb("blocks", [P, GROUPS // 2, QUADS, DA])
        gain = sb("gain", [P, E])
        shift = sb("shift", [P, BATCH, E])
        obias = sb("obias", [P, BATCH, E])
        neg_half = sb("neg_half", [P, BATCH])
        half4 = sb("half4", [P, 4])

        wT = [sb(f"wT{m}", [P, 2, GROUPS, E], F16) for m in range(4)]
        sumsq = sb("sumsq", [P, 4, GROUPS])
        norm2 = sb("norm2", [P, 4])
        norm2_all = sb("norm2_all", [P, 4])
        norm = sb("norm", [P, 4])
        pow2 = sb("pow2", [P, 4])
        rpow2 = sb("rpow2", [P, 4])
        w_scale = sb("w_scale", [P, 4])
        inv_scale = sb("inv_scale", [P, 2])
        f_bound = sb("f_bound", [P, 2])
        f_scale = sb("f_scale", [P, 2])
        den_eps = sb("den_eps", [P, 1])
        out_scale = sb("out_scale", [P, 1])

        X = sb("X", [P, 2, BATCH, E])
        XB = sb("XB", [P, BATCH, E])
        GAINED = sb("GAINED", [P, BATCH, E])
        X1 = sb("X1", [P, BATCH, E])
        X1BO = sb("X1BO", [P, 2, BATCH, E])
        XN = sb("XN", [P, BATCH, E])
        raw = sb("raw", [P, BATCH, 6])
        stat0 = sb("stat0", [P, BATCH, 2])
        stat1 = sb("stat1", [P, BATCH, 2])
        stat2 = sb("stat2", [P, BATCH, 2])
        var0 = sb("var0", [P, BATCH])
        var1 = sb("var1", [P, BATCH])
        var2 = sb("var2", [P, BATCH])
        rstd0 = sb("rstd0", [P, BATCH])
        rstd1 = sb("rstd1", [P, BATCH])
        rstd2 = sb("rstd2", [P, BATCH])
        minus_one = sb("minus_one", [P, BATCH])
        neg_mean = sb("neg_mean", [P, BATCH])
        offset1 = sb("offset1", [P, BATCH])
        XT = sb("XT", [P, 2, GROUPS, TOK], F16)
        PHI = sb("PHI", [P, 4, E])
        RELU = sb("RELU", [P, 2, E])
        QT = [sb(f"QT{p}", [P, 2, GROUPS, TOK], F16) for p in range(2)]
        KT = sb("KT", [P, 2, GROUPS, TOK], F16)
        QS = [sb(f"QS{p}", [P, H, TOK], F16) for p in range(2)]
        KS = [sb(f"KS{p}", [P, H, TOK], F16) for p in range(2)]
        KN = [sb(f"KN{p}", [P, BATCH, 2, E], F16) for p in range(2)]
        VN = [sb(f"VN{p}", [P, BATCH, 2, H, DA], F16) for p in range(2)]
        AM = sb("AM", [P, 4, E])
        A = sb("A", [P, BATCH, 2, GROUPS, E], F16)
        wnat = [A[:, m].rearrange("p f g q -> p (f g q)").bitcast(F32).rearrange("p (c e) -> p c e", c=GROUPS)
                for m in range(2)]
        wnat += [QS[m][:].rearrange("p h t -> p (h t)").bitcast(F32).rearrange("p (c e) -> p c e", c=GROUPS)
                 for m in range(2)]
        DELTA = sb("DELTA", [P, 2, 2 * QUADS * DA])
        S = sb("S", [P, BATCH, 2, 2 * QUADS * DA])
        SH = sb("SH", [P, BATCH, 2, 2, 2 * QUADS * DA], F16)
        DEN = sb("DEN", [P, 2, H // 2])
        RDEN = sb("RDEN", [P, 2, H // 2])
        ATTN = sb("ATTN", [P, BATCH, E])
        AT = sb("AT", [P, BATCH, 2, E], F16)
        X2 = sb("X2", [P, BATCH, E])
        Y = sb("Y", [P, BATCH, E])
        raw2 = sb("raw2", [P, BATCH, 6])
        wsq = Y[:, 0]

        TP = [ps(f"TP{i}") for i in range(2)]
        PJ = [ps(f"PJ{i}") for i in range(2)]
        SC = [ps(f"SC{i}") for i in range(2)]
        AV = [ps(f"AV{i}") for i in range(2)]
        TP16 = [t[:].bitcast(F16) for t in TP]

        w_loaded = [sem(f"w_loaded{m}") for m in range(4)]
        norm_consts_loaded = sem("norm_consts_loaded")
        obias_loaded = sem("obias_loaded")
        consts_done = sem("consts_done")
        pool_step = sem("pool_step")
        w_summed = sem("w_summed")
        norm2_done = sem("norm2_done")
        norm2_reduced = sem("norm2_reduced")
        norm_done = sem("norm_done")
        scales_done = sem("scales_done")
        dve_setup = sem("dve_setup")
        wT_filled = sem("wT_filled")
        wT_hi = sem("wT_hi")
        wT_lo = sem("wT_lo")
        consts_scaled = sem("consts_scaled")
        zeroed = sem("zeroed")

        x_loaded = [sem(f"x_loaded{p}") for p in range(2)]
        stat0_raw, stat0_done = sig("stat0_raw", 2), sig("stat0_done", 2)
        stat1_raw, stat1_done = sig("stat1_raw", 2), sig("stat1_done", 2)
        stat2_raw, stat2_done = sig("stat2_raw", 2), sig("stat2_done", 2)
        var0_done, var1_done, var2_done = sig("var0_done", 1), sig("var1_done", 1), sig("var2_done", 1)
        neg_mean_done, offset1_done = sig("neg_mean_done", 1), sig("offset1_done", 1)
        rstd0_done, rstd1_done, rstd2_done = sig("rstd0_done", 1), sig("rstd1_done", 1), sig("rstd2_done", 1)
        xb_done, x1bo_done, x2b_done = sig("xb_done", 1), sig("x1bo_done", 1), sig("x2b_done", 1)
        x_gained, x1_done, xn_done = sig("x_gained", 2), sig("x1_done", 2), sig("xn_done", 2)
        xT_filled, xT_hi, xT_lo = sig("xT_filled", 2), sig("xT_hi", 2), sig("xT_lo", 2)
        q_filled, q_exp, q_relu = sig("q_filled", 2), sig("q_exp", 2), sig("q_relu", 2)
        q_phi, q_hi, q_lo = sig("q_phi", 2), sig("q_hi", 2), sig("q_lo", 2)
        k_filled, k_exp, k_relu = sig("k_filled", 2), sig("k_exp", 2), sig("k_relu", 2)
        k_phi, k_hi, k_lo = sig("k_phi", 2), sig("k_hi", 2), sig("k_lo", 2)
        v_filled, v_hi, v_lo = sig("v_filled", 2), sig("v_hi", 2), sig("v_lo", 2)
        kT_filled, kT_copied = sig("kT_filled", 2), sig("kT_copied", 2)
        q_stacked = [sem(f"q_stacked{p}") for p in range(2)]
        k_stacked = [sem(f"k_stacked{p}") for p in range(2)]
        sc_filled, sc_masked = sig("sc_filled", 8), sig("sc_masked", 4)
        sc_copied, sc_cut = sig("sc_copied", 4), sig("sc_cut", 4)
        a_hi, a_lo = sig("a_hi", 8), sig("a_lo", 8)
        av_filled, den_done, rden_done, attn_done = (sig("av_filled", 4), sig("den_done", 4),
                                                     sig("rden_done", 4), sig("attn_done", 4))
        st_filled, delta_done = sig("st_filled", 4), sig("delta_done", 4)
        s_added, s_hi, s_lo = sig("s_added", 4), sig("s_hi", 2), sig("s_lo", 2)
        attnT_filled, attnT_hi, attnT_lo = sig("attnT_filled", 2), sig("attnT_hi", 2), sig("attnT_lo", 2)
        out_filled, x2_done = sig("out_filled", 2), sig("x2_done", 2)
        x2_gained, y_done = sig("x2_gained", 2), sig("y_done", 2)
        y_stored = sig("y_stored", 1, 16)
        a_lo_even = sem("a_lo_even")
        last_var, last_rstd, last_shifted = sem("last_var"), sem("last_rstd"), sem("last_shifted")

        steps = CHUNKS
        weights = (Wq, Wk, Wv, Wo)
        W_ORDER = (1, 0, 2, 3)
        W_BANKS = PJ + (SC + AV) * 3 + SC
        W_REUSE = len(PJ + SC + AV)

        class Step:

            def __init__(self, t, r):
                self.t, self.r = t, r
                self.number = isinstance(t, int)

            def chunk(self, ahead):
                return self.t * 2 + (self.r + ahead)

            def parity(self, ahead):
                return (self.r + ahead) % 2

            def pair(self, ahead, by):
                return self.t * by + ((self.r + ahead) // 2 + 1) * by

            def has(self, ahead):
                return not self.number or 0 <= self.chunk(ahead) < steps

        def run_first(body):
            for s in (-3, -2):
                body(Step(0, s))

        def run(eng, body):
            for s in range(-1, 2):
                body(Step(0, s))
            with eng.Fori(1, steps // 2 - 2) as t:
                body(Step(t, 0))
                body(Step(t, 1))
            for s in range(steps - 4, steps):
                body(Step(0, s))

        def pair_wait(eng, sems, st, ahead, by):
            eng.wait_ge(sems[st.parity(ahead)], st.pair(ahead, by))

        passed = {e: sem(f"passed_{e}") for e in ("sp", "pool", "dve")}

        def stand(eng, name):
            eng.sem_inc(passed[name], 1)

        block = ctx.enter_context(nc.Block())

        @block.sync
        def _(sp):
            def load_x(i):
                sp.dma_start(X[:, i], x[:, i * C:(i + 1) * C, :].rearrange("b p e -> p b e")).then_inc(x_loaded[i], 16)

            load_x(0)
            sp.dma_start(gain[:], ln_g.rearrange("(a n) -> a n", a=1).to_broadcast([P, E])).then_inc(norm_consts_loaded, 16)
            sp.dma_start(shift[:, 0], ln_b.rearrange("(a n) -> a n", a=1).to_broadcast([P, E])).then_inc(norm_consts_loaded, 16)
            for m in W_ORDER:
                sp.dma_start(wnat[m], weights[m].rearrange("(c p) e -> p c e", p=P)).then_inc(w_loaded[m], 16)
            for b in range(BATCH):
                sp.dma_start(obias[:, b], attn_bo.rearrange("(a n) -> a n", a=1).to_broadcast([P, E])).then_inc(obias_loaded, 16)
            load_x(1)

            def body(st):
                n, p = st.chunk(1), st.parity(1)
                if st.has(4) and (not st.number or st.chunk(4) >= 2):
                    wait(sp, x_gained, st.chunk(2), 1)
                    stand(sp, "sp")
                    wait(sp, xb_done, st.chunk(2))
                    stand(sp, "sp")
                    i = st.chunk(4)
                    start = i * C
                    sp.dma_start(X[:, st.parity(4)], x[:, bass.ds(start, C), :].rearrange("b p e -> p b e")).then_inc(x_loaded[st.parity(4)], 16)
                if st.has(1):
                    if st.has(-1):
                        wait(sp, sc_filled, st.chunk(-1), 7)
                    for half, j in sorted((half, j) for j, half in enumerate(Q_STACK)):
                        wait(sp, q_lo if half == LO else q_hi, n, 1)
                        for h in range(QUADS):
                            sp.dma_start(QS[p][D * j:D * j + D, h::QUADS, :],
                                         QT[p][D * h:D * h + D, half]).then_inc(q_stacked[p], 16)
                    wait(sp, kT_copied, n, 1)
                    for j, half in enumerate(K_STACK):
                        for h in range(QUADS):
                            sp.dma_start(KS[p][D * j:D * j + D, h::QUADS, :],
                                         KT[D * h:D * h + D, half]).then_inc(k_stacked[p], 16)
                if st.has(-1):
                    i = st.chunk(-1)
                    wait(sp, y_done, i, 1)
                    stand(sp, "sp")
                    sp.dma_start(out[:, bass.ds(i * C, C), :].rearrange("b p e -> p b e"), Y[:]).then_inc(y_stored.sem, 16)
                if st.has(0) and not st.has(1):
                    i = st.chunk(0)
                    for b in range(BATCH):
                        wait(sp, y_done, i, b)
                        sp.dma_start(out[b, i * C:(i + 1) * C, :], Y[:, b]).then_inc(y_stored.sem, 16)

            run_first(body)
            run(sp, body)
            sp.wait_ge(y_stored.sem, y_stored.at(steps - 2) + 16 * BATCH)

        @block.gpsimd
        def _(pool):
            g = nc.gpsimd
            count = [0]

            def link(ins):
                count[0] += 1
                ins.then_inc(pool_step, 1)
                pool.wait_ge(pool_step, count[0])

            g.memset(neg_half[:], -0.5)
            g.memset(half4[:], 0.5)
            g.memset(minus_one[:], -1.0)
            g.memset(ident[:], 0.0)
            link(g.memset(causal[:], SUM_DOWN))
            g.memset(blocks[:], SUM_DOWN)
            link(g.affine_select(out=ident[:], in_=ident[:], compare_op=ALU.not_equal, fill=1.0, base=0,
                                 pattern=[[-1, P]], channel_multiplier=1))
            link(g.affine_select(out=causal[:], in_=causal[:], compare_op=ALU.is_ge, fill=0.0, base=0,
                                 pattern=[[1, P]], channel_multiplier=-1))
            link(g.affine_select(out=blocks[:], in_=blocks[:], compare_op=ALU.is_ge, fill=0.0, base=0,
                                 pattern=[[0, 2], [-D, QUADS], [0, DA]], channel_multiplier=1))
            link(g.affine_select(out=blocks[:], in_=blocks[:], compare_op=ALU.is_ge, fill=0.0, base=D - 1,
                                 pattern=[[0, 2], [D, QUADS], [0, DA]], channel_multiplier=-1))
            g.tensor_copy(ident16[:], ident[:]).then_inc(consts_done, 1)
            pool.wait_ge(consts_scaled, 3)
            pool.wait_ge(zeroed, 1)

            def rstd(var, var_done, rstd_, rstd_done, stat, stat_done, i, prev, double):
                if prev is not None:
                    wait(pool, rstd_done, prev)
                wait(pool, stat_done, i, 1)
                a, c = (1.0 + EPS, EPS * EPS) if double else (1.0, EPS)
                stand(pool, "pool")
                g.tensor_scalar(var[:], stat[:, :, 1], a, c, ALU.mult, ALU.add).then_inc(var_done.sem, 1)
                wait(pool, var_done, i)
                g.tensor_tensor(rstd_[:], var[:], neg_half[:], ALU.pow).then_inc(rstd_done.sem, 1)

            def norms(pair):
                at = slice(2 * pair, 2 * pair + 2)
                pool.wait_ge(norm2_done, pair + 1)
                g.partition_all_reduce(norm2_all[:, at], norm2[:, at], P, RMAX).then_inc(norm2_reduced, 1)
                pool.wait_ge(norm2_reduced, pair + 1)
                g.tensor_tensor(norm[:, at], norm2_all[:, at], half4[:, at], ALU.pow).then_inc(norm_done, 1)

            def body(st):
                s, n, f, back = st.chunk(0), st.chunk(1), st.chunk(2), st.chunk(-1)

                def x1_bias():
                    if not ATTEND:
                        pool.wait_ge(obias_loaded, 16 * BATCH)
                    wait(pool, x1_done, n, 1)
                    if st.has(-1):
                        wait(pool, x2_done, back, 1)
                    g.tensor_tensor(X1BO[:, st.parity(1)], X1[:], obias[:], ALU.add).then_inc(x1bo_done.sem, 1)

                def x_shift():
                    pair_wait(pool, x_loaded, st, 3, 16)
                    if st.has(2):
                        wait(pool, x1_done, f, 1)
                    g.tensor_tensor(XB[:], X[:, st.parity(3)], shift[:], ALU.add).then_inc(xb_done.sem, 1)

                def x2_shift():
                    wait(pool, x2_gained, back, 1)
                    g.tensor_tensor(X2[:], X2[:], shift[:], ALU.add).then_inc(x2b_done.sem, 1)

                def norm_offset():
                    wait(pool, stat1_done, f, 1)
                    if st.has(1):
                        wait(pool, offset1_done, n)
                        wait(pool, xn_done, n, 1)
                    g.tensor_tensor(neg_mean[:], stat1[:, :, 0], minus_one[:], ALU.mult).then_inc(neg_mean_done.sem, 1)
                    wait(pool, neg_mean_done, f)
                    wait(pool, rstd1_done, f)
                    g.tensor_tensor(offset1[:], neg_mean[:], rstd1[:], ALU.mult).then_inc(offset1_done.sem, 1)

                def cut(b, hg):
                    k = b * GROUPS + hg
                    wait(pool, sc_copied, s, k // 2)
                    stand(pool, "pool")
                    am = AM[:, k % 4].rearrange("p (h q) -> p h q", h=QUADS)
                    g.affine_select(out=am, in_=am, compare_op=ALU.is_ge, fill=0.0, base=0,
                                    pattern=[[0, QUADS], [1, C]], channel_multiplier=-1).then_inc(sc_cut.sem, 1)

                def split_a(b, hg):
                    k = b * GROUPS + hg
                    if not PROJECT and hg % 2 == 0:
                        return
                    wait(pool, a_hi, s, k)
                    g.tensor_tensor(A[:, b, LO, hg], AM[:, k % 4], A[:, b, HI, hg],
                                    ALU.subtract).then_inc(a_lo.sem, 1 if PROJECT else 2)

                def add_s(b, hf):
                    wait(pool, delta_done, s, 2 * b + hf)
                    if hf == 0 and st.has(-1):
                        wait(pool, s_hi, back, b)
                        wait(pool, s_lo, back, b)
                    g.tensor_tensor(S[:, b, hf], S[:, b, hf], DELTA[:, hf], ALU.add).then_inc(s_added.sem, 1)

                def split_s(b):
                    wait(pool, s_hi, s, b)
                    g.tensor_tensor(SH[:, b, LO], S[:, b], SH[:, b, HI], ALU.subtract).then_inc(s_lo.sem, 1)

                def finish_last(b):
                    if b == 0:
                        wait(pool, y_done, back, 1)
                    wait(pool, stat2_done, s, b)
                    g.tensor_scalar(var2[:, b:b + 1], stat2[:, b, 1:2], 1.0 + EPS, EPS * EPS,
                                    ALU.mult, ALU.add).then_inc(last_var, 1)
                    pool.wait_ge(last_var, b + 1)
                    g.tensor_tensor(rstd2[:, b:b + 1], var2[:, b:b + 1], neg_half[:, b:b + 1],
                                    ALU.pow).then_inc(last_rstd, 1)
                    wait(pool, x2_gained, s, b)
                    g.tensor_tensor(X2[:, b], X2[:, b], shift[:, b], ALU.add).then_inc(last_shifted, 1)

                def rstd0_of_x():
                    if PROJECT:
                        wait(pool, x1_done, n, 1)
                    rstd(var0, var0_done, rstd0, rstd0_done, stat0, stat0_done, f, n if PROJECT else None, True)

                def rstd1_of_x1():
                    if PROJECT:
                        wait(pool, xn_done, n, 1)
                    rstd(var1, var1_done, rstd1, rstd1_done, stat1, stat1_done, f, n if PROJECT else None, False)

                def rstd2_of_x2():
                    rstd(var2, var2_done, rstd2, rstd2_done, stat2, stat2_done, back,
                         st.chunk(-2) if st.has(-2) else None, True)

                PROJECT, ATTEND, FRONT, FINISH = st.has(1), st.has(0), st.has(2), st.has(-1)
                if ATTEND and not PROJECT:
                    rstd2_of_x2()
                    cut(0, 1)
                    split_a(0, 1)
                    cut(0, 3)
                    cut(1, 1)
                    split_a(0, 3)
                    split_a(1, 1)
                    cut(1, 3)
                    split_a(1, 3)
                    x2_shift()
                    finish_last(0)
                    finish_last(1)
                    return
                if PROJECT:
                    x1_bias()
                if FRONT:
                    rstd0_of_x()
                if FRONT and not PROJECT:
                    norms(0)
                if ATTEND:
                    cut(0, 1)
                if FINISH:
                    rstd2_of_x2()
                if ATTEND:
                    split_a(0, 0)
                    split_a(0, 1)
                    cut(0, 3)
                    split_a(0, 2)
                    split_a(0, 3)
                if FRONT:
                    rstd1_of_x1()
                    norm_offset()
                if FRONT and not PROJECT:
                    norms(1)
                if ATTEND:
                    cut(1, 1)
                    split_a(1, 0)
                    split_a(1, 1)
                    cut(1, 3)
                    split_a(1, 2)
                    split_a(1, 3)
                    add_s(0, 0)
                    add_s(0, 1)
                if FINISH:
                    x2_shift()
                if ATTEND:
                    add_s(1, 0)
                    add_s(1, 1)
                if st.has(3):
                    x_shift()
                if ATTEND:
                    split_s(0)
                    split_s(1)

            run_first(body)
            run(pool, body)

        @block.scalar
        def _(act):
            a = nc.scalar

            def square(j):
                m = W_ORDER[j]
                act.wait_ge(w_loaded[m], 16)
                for c in range(GROUPS):
                    a.activation(wsq, wnat[m][:, c], ACT.Square, accum_out=sumsq[:, m, c:c + 1]).then_inc(w_summed, 1)
                    act.wait_ge(w_summed, j * GROUPS + c + 1)

            def w_half(j):
                m = W_ORDER[j]
                act.wait_ge(scales_done, j // 2 + 1)
                for c in range(GROUPS):
                    k = j * GROUPS + c
                    act.wait_ge(wT_filled, k + 1)
                    a.activation(wT[m][:, HI, c], W_BANKS[k][:], ACT.Copy, scale=w_scale[:, m:m + 1]).then_inc(wT_hi, 1)

            square(0)
            square(1)

            def body(st):
                s, n, f, back = st.chunk(0), st.chunk(1), st.chunk(2), st.chunk(-1)
                PROJECT, ATTEND, FRONT, FINISH = st.has(1), st.has(0), st.has(2), st.has(-1)

                def normalise(b):
                    wait(act, offset1_done, f)
                    if PROJECT and b == 0:
                        wait(act, xT_filled, n, 1)
                    a.activation(XN[:, b], X1[:, b], ACT.Identity, bias=offset1[:, b:b + 1],
                                 scale=rstd1[:, b:b + 1]).then_inc(xn_done.sem, 1)

                def x_half(b):
                    wait(act, xT_filled, f, b)
                    if PROJECT:
                        wait(act, v_filled, n, 1)
                    a.activation(XT[:, HI, :, b * C:(b + 1) * C], TP[b][:].rearrange("p (c t) -> p c t", c=GROUPS),
                                 ACT.Copy, scale=X_UP).then_inc(xT_hi.sem, 1)

                def exp_relu_k(b):
                    wait(act, k_filled, n, b)
                    if ATTEND:
                        wait(act, k_lo, s, b)
                        wait(act, q_phi, s, b)
                    a.activation(PHI[:, b], PJ[b][:], ACT.Exp, scale=inv_scale[:, 1:2]).then_inc(k_exp.sem, 1)
                    a.activation(RELU[:, b], PJ[b][:], ACT.Relu, scale=inv_scale[:, 1:2]).then_inc(k_relu.sem, 1)

                def exp_relu_q(pr):
                    wait(act, q_filled, n, pr)
                    if ATTEND:
                        wait(act, q_lo, s, pr)
                    wait(act, k_phi, n, pr)
                    a.activation(PHI[:, 2 + pr], PJ[pr][:], ACT.Exp, scale=inv_scale[:, 0:1]).then_inc(q_exp.sem, 1)
                    a.activation(RELU[:, pr], PJ[pr][:], ACT.Relu, scale=inv_scale[:, 0:1]).then_inc(q_relu.sem, 1)

                def q_half(pr):
                    wait(act, q_phi, n, pr)
                    if FINISH and pr == 0:
                        wait(act, av_filled, back, 3)
                        pair_wait(act, q_stacked, st, -1, 16 * RESTACKS)
                    a.activation(QT[st.parity(1)][:, HI, 2 * pr:2 * pr + 2], PHI[:, 2 + pr].rearrange("p (g t) -> p g t", g=2),
                                 ACT.Copy, scale=f_scale[:, 0:1]).then_inc(q_hi.sem, 1)

                def k_half(b):
                    wait(act, k_phi, n, b)
                    if FINISH:
                        wait(act, st_filled, back, 2 * b + 1)
                    a.activation(KN[st.parity(1)][:, b, HI], PHI[:, b], ACT.Copy, scale=f_scale[:, 1:2]).then_inc(k_hi.sem, 1)

                def copy_scores(b, hg):
                    k = b * GROUPS + hg
                    wait(act, sc_filled, s, k)
                    if k >= 4:
                        wait(act, a_lo, s, k - 4)
                    elif FINISH:
                        wait(act, a_lo, back, k + 4)
                    a.activation(AM[:, k % 4], SC[hg % 2][:], ACT.Copy, scale=SUM_DOWN).then_inc(sc_copied.sem, 1)

                def split_a(b, hg):
                    k = b * GROUPS + hg
                    wait(act, sc_cut if hg % 2 else sc_masked, s, k // 2)
                    if hg == 0 and FINISH:
                        wait(act, av_filled, back, 2 * b + 1)
                    a.activation(A[:, b, HI, hg], AM[:, k % 4], ACT.Copy).then_inc(a_hi.sem, 1)

                def kT(b):
                    wait(act, kT_filled, n, b)
                    if ATTEND and b == 0:
                        pair_wait(act, k_stacked, st, 0, 16 * RESTACKS)
                    a.activation(KT[:, :, :, b * C:(b + 1) * C],
                                 TP16[b].rearrange("p (f c t) -> p f c t", f=2, c=GROUPS),
                                 ACT.Copy).then_inc(kT_copied.sem, 1)

                def v_half(b):
                    wait(act, v_filled, n, b)
                    if FINISH:
                        wait(act, st_filled, back, 2 * b + 1)
                    a.activation(VN[st.parity(1)][:, b, HI, :, 0:D], PJ[b][:].rearrange("p (h d) -> p h d", h=H),
                                 ACT.Copy, scale=V_SCALE).then_inc(v_hi.sem, 1)

                def attn_half(b):
                    wait(act, attnT_filled, s, b)
                    if FINISH:
                        wait(act, out_filled, back, b)
                    a.activation(AT[:, b, HI], TP[b][:], ACT.Copy, scale=ATTN_UP).then_inc(attnT_hi.sem, 1)

                def s_half(b):
                    wait(act, s_added, s, 2 * b + 1)
                    wait(act, av_filled, s, 2 * b + 1)
                    a.activation(SH[:, b, HI], S[:, b], ACT.Copy).then_inc(s_hi.sem, 1)

                if FRONT and not PROJECT:
                    square(2)
                    normalise(0)
                    normalise(1)
                    w_half(0)
                    x_half(0)
                    x_half(1)
                    square(3)
                    w_half(1)
                    return
                if ATTEND and not PROJECT:
                    copy_scores(0, 1)
                    split_a(0, 0)
                    split_a(0, 1)
                    copy_scores(0, 3)
                    split_a(0, 2)
                    copy_scores(1, 1)
                    split_a(0, 3)
                    split_a(1, 0)
                    split_a(1, 1)
                    copy_scores(1, 3)
                    split_a(1, 2)
                    split_a(1, 3)
                    attn_half(0)
                    attn_half(1)
                    return
                if PROJECT:
                    exp_relu_k(0)
                    exp_relu_k(1)
                if PROJECT and not FINISH:
                    k_half(0)
                    k_half(1)
                if PROJECT and not ATTEND:
                    w_half(2)
                if ATTEND:
                    copy_scores(0, 1)
                    split_a(0, 0)
                if PROJECT and FINISH:
                    k_half(0)
                    k_half(1)
                if ATTEND:
                    split_a(0, 1)
                    copy_scores(0, 3)
                if PROJECT:
                    exp_relu_q(0)
                if ATTEND:
                    split_a(0, 2)
                if PROJECT:
                    exp_relu_q(1)
                if ATTEND:
                    split_a(0, 3)
                if PROJECT:
                    q_half(0)
                    q_half(1)
                if ATTEND:
                    copy_scores(1, 1)
                if PROJECT:
                    kT(0)
                if ATTEND:
                    split_a(1, 0)
                    split_a(1, 1)
                if FRONT and PROJECT and not ATTEND:
                    normalise(0)
                    normalise(1)
                if PROJECT:
                    kT(1)
                if ATTEND:
                    copy_scores(1, 3)
                if PROJECT:
                    v_half(0)
                if ATTEND:
                    split_a(1, 2)
                    split_a(1, 3)
                if PROJECT:
                    v_half(1)
                if ATTEND:
                    attn_half(0)
                if FRONT and ATTEND:
                    normalise(0)
                    normalise(1)
                if ATTEND:
                    attn_half(1)
                if FRONT:
                    x_half(0)
                if ATTEND:
                    s_half(0)
                    s_half(1)
                if FRONT:
                    x_half(1)
                if PROJECT and not ATTEND:
                    w_half(3)

            run_first(body)
            run(act, body)

        @block.vector
        def _(dve):
            v = nc.vector
            count = [0]

            def link(ins):
                count[0] += 1
                ins.then_inc(dve_setup, 1)
                dve.wait_ge(dve_setup, count[0])

            link(v.memset(S[:], 0.0))
            link(v.memset(SH[:], 0.0))
            for p in range(2):
                link(v.memset(VN[p][:, :, HI, :, D:DA], ATTN_UP))
                link(v.memset(VN[p][:, :, LO, :, D:DA], 0.0))
            dve.wait_ge(norm_consts_loaded, 16 * 2)
            v.tensor_scalar(shift[:, 1], shift[:, 0], 0.5, None, ALU.mult).then_inc(consts_scaled, 1)
            v.tensor_scalar(gain[:], gain[:], 0.5, None, ALU.mult).then_inc(consts_scaled, 1)
            dve.wait_ge(consts_scaled, 1)
            v.tensor_copy(shift[:, 0], shift[:, 1]).then_inc(consts_scaled, 1)
            dve.wait_ge(consts_scaled, 3)
            v.memset(DEN[:], 1.0).then_inc(zeroed, 1)
            dve.wait_ge(zeroed, 1)
            dve.wait_ge(consts_done, 1)

            def row_sums(pair):
                at = slice(2 * pair, 2 * pair + 2)
                dve.wait_ge(w_summed, (pair + 1) * 2 * GROUPS)
                link(v.tensor_reduce(norm2[:, at], sumsq[:, at], mybir.AxisListType.X, ALU.max))
                v.tensor_scalar(norm2[:, at], norm2[:, at], 1e-30, None, ALU.max).then_inc(norm2_done, 1)

            def scales(pair):
                at = slice(2 * pair, 2 * pair + 2)
                dve.wait_ge(norm_done, pair + 1)
                link(v.tensor_scalar(pow2[:, at].bitcast(U32), norm[:, at].bitcast(U32), 0x7F800000, None, ALU.bitwise_and))
                link(v.reciprocal(rpow2[:, at], pow2[:, at]))
                link(v.tensor_scalar(w_scale[:, at], rpow2[:, at], TOP, None, ALU.mult))
                if pair == 0:
                    link(v.tensor_scalar(inv_scale[:], pow2[:, at], 1.0 / (TOP * X_UP), None, ALU.mult))
                    link(v.tensor_scalar(f_bound[:], pow2[:, at], 64.0, 1.0, ALU.mult, ALU.max))
                    link(v.reciprocal(f_scale[:], f_bound[:]))
                    link(v.tensor_scalar(f_scale[:], f_scale[:], TOP, None, ALU.mult))
                    link(v.tensor_tensor(den_eps[:], f_scale[:, 0:1], f_scale[:, 1:2], ALU.mult))
                    v.tensor_scalar(den_eps[:], den_eps[:], SUM_DOWN * ATTN_UP, EPS, ALU.mult, ALU.mult).then_inc(scales_done, 1)
                else:
                    link(v.tensor_tensor(out_scale[:], pow2[:, 2:3], pow2[:, 3:4], ALU.mult))
                    v.tensor_scalar(out_scale[:], out_scale[:], 1.0 / (TOP * X_UP * V_SCALE * TOP), None, ALU.mult).then_inc(scales_done, 1)
                dve.wait_ge(scales_done, pair + 1)

            def w_low(j):
                m = W_ORDER[j]
                for c in range(GROUPS):
                    k = j * GROUPS + c
                    dve.wait_ge(wT_hi, k + 1)
                    v.scalar_tensor_tensor(wT[m][:, LO, c], W_BANKS[k][:], w_scale[:, m:m + 1], wT[m][:, HI, c],
                                           ALU.mult, ALU.subtract).then_inc(wT_lo, 1)

            def stats(src, rawt, stat, raw_sig, done_sig, i, b):
                v.bn_stats(rawt[:, b], src).then_inc(raw_sig.sem, 1)
                wait(dve, raw_sig, i, b)
                stand(dve, "dve")
                v.bn_aggr(stat[:, b], rawt[:, b]).then_inc(done_sig.sem, 1)

            def body(st):
                s, n, f, back = st.chunk(0), st.chunk(1), st.chunk(2), st.chunk(-1)
                PROJECT, ATTEND, FRONT, FINISH = st.has(1), st.has(0), st.has(2), st.has(-1)

                def front_stats(b):
                    if b == 0:
                        pair_wait(dve, x_loaded, st, 2, 16)
                        if st.has(1):
                            wait(dve, var0_done, n)
                            wait(dve, x_gained, n, 1)
                            wait(dve, stat1_done, n, 1)
                    stats(X[:, st.parity(2), b], raw, stat0, stat0_raw, stat0_done, f, b)

                def front_gain(b):
                    wait(dve, stat0_done, f, b)
                    if st.has(-2):
                        wait(dve, y_done, st.chunk(-2), b)
                    elif PROJECT:
                        wait(dve, x1_done, n, b)
                    v.scalar_tensor_tensor(GAINED[:, b], X[:, st.parity(2), b], stat0[:, b, 0:1], gain[:],
                                           ALU.subtract, ALU.mult).then_inc(x_gained.sem, 1)

                def front_x1(b):
                    wait(dve, x_gained, f, b)
                    if b == 0:
                        wait(dve, rstd0_done, f)
                        wait(dve, xb_done, f)
                        if st.has(1):
                            wait(dve, x1bo_done, n)
                            wait(dve, xn_done, n, 1)
                    v.scalar_tensor_tensor(X1[:, b], GAINED[:, b], rstd0[:, b:b + 1], XB[:, b],
                                           ALU.mult, ALU.add).then_inc(x1_done.sem, 1)

                def front_stats1(b):
                    wait(dve, x1_done, f, b)
                    if b == 0 and st.has(1):
                        wait(dve, var1_done, n)
                    stats(X1[:, b], raw, stat1, stat1_raw, stat1_done, f, b)

                def x_low(b):
                    wait(dve, xT_hi, f, b)
                    v.scalar_tensor_tensor(XT[:, LO, :, b * C:(b + 1) * C],
                                           TP[b][:].rearrange("p (c t) -> p c t", c=GROUPS), X_UP,
                                           XT[:, HI, :, b * C:(b + 1) * C],
                                           ALU.mult, ALU.subtract).then_inc(xT_lo.sem, 1)

                def mask(b, hg):
                    k = b * GROUPS + hg
                    wait(dve, sc_filled, s, k)
                    if k >= 4 and not PROJECT:
                        dve.wait_ge(a_lo_even, k // 2 - 1)
                    elif k >= 4:
                        wait(dve, a_lo, s, k - 4)
                    elif FINISH:
                        wait(dve, a_lo, back, k + 4)
                    v.tensor_tensor(AM[:, k % 4].rearrange("p (h q) -> p h q", h=QUADS),
                                    SC[hg % 2][:].rearrange("p (h q) -> p h q", h=QUADS),
                                    causal[:].unsqueeze(1).to_broadcast([P, QUADS, C]),
                                    ALU.mult).then_inc(sc_masked.sem, 1)

                def split_a(b, hg):
                    k = b * GROUPS + hg
                    wait(dve, a_hi, s, k)
                    v.tensor_tensor(A[:, b, LO, hg], AM[:, k % 4], A[:, b, HI, hg], ALU.subtract).then_inc(a_lo_even, 1)

                def phi_q(pr):
                    wait(dve, q_relu, n, pr)
                    v.scalar_tensor_tensor(PHI[:, 2 + pr], PHI[:, 2 + pr], 1.0, RELU[:, pr],
                                           ALU.min, ALU.add).then_inc(q_phi.sem, 1)

                def low_q(pr):
                    wait(dve, q_hi, n, pr)
                    v.scalar_tensor_tensor(QT[st.parity(1)][:, LO, 2 * pr:2 * pr + 2],
                                           PHI[:, 2 + pr].rearrange("p (g t) -> p g t", g=2), f_scale[:, 0:1],
                                           QT[st.parity(1)][:, HI, 2 * pr:2 * pr + 2],
                                           ALU.mult, ALU.subtract).then_inc(q_lo.sem, 1)

                def phi_k(b):
                    wait(dve, k_relu, n, b)
                    v.scalar_tensor_tensor(PHI[:, b], PHI[:, b], 1.0, RELU[:, b],
                                           ALU.min, ALU.add).then_inc(k_phi.sem, 1)

                def low_k(b):
                    wait(dve, k_hi, n, b)
                    v.scalar_tensor_tensor(KN[st.parity(1)][:, b, LO], PHI[:, b], f_scale[:, 1:2],
                                           KN[st.parity(1)][:, b, HI], ALU.mult, ALU.subtract).then_inc(k_lo.sem, 1)

                def low_v(b):
                    wait(dve, v_hi, n, b)
                    v.scalar_tensor_tensor(VN[st.parity(1)][:, b, LO, :, 0:D], PJ[b][:].rearrange("p (h d) -> p h d", h=H),
                                           V_SCALE, VN[st.parity(1)][:, b, HI, :, 0:D],
                                           ALU.mult, ALU.subtract).then_inc(v_lo.sem, 1)

                def quotient(b, hf):
                    k = 2 * b + hf
                    wait(dve, av_filled, s, k)
                    av = AV[hf][:, 0:2 * QUADS * DA].rearrange("p (h d) -> p h d", d=DA)
                    if b == 1:
                        wait(dve, attn_done, s, hf)
                    elif FINISH:
                        wait(dve, attn_done, back, 2 + hf)
                    v.tensor_scalar(DEN[:, hf], av[:, :, D], den_eps[:], None, ALU.add).then_inc(den_done.sem, 1)
                    wait(dve, den_done, s, k)
                    v.reciprocal(RDEN[:, hf], DEN[:, hf]).then_inc(rden_done.sem, 1)
                    wait(dve, rden_done, s, k)
                    if FINISH and hf == 0:
                        wait(dve, attnT_filled, back, b)
                    v.tensor_tensor(ATTN[:, b, hf * (E // 2):(hf + 1) * (E // 2)].rearrange("p (h d) -> p h d", d=D),
                                    av[:, :, 0:D], RDEN[:, hf].unsqueeze(2).to_broadcast([P, H // 2, D]),
                                    ALU.mult).then_inc(attn_done.sem, 1)

                def delta(b, hf):
                    k = 2 * b + hf
                    wait(dve, st_filled, s, k)
                    if b == 1:
                        wait(dve, s_added, s, hf)
                    elif FINISH:
                        wait(dve, s_added, back, 2 + hf)
                    v.tensor_tensor(DELTA[:, hf], PJ[hf][:, 0:2 * QUADS * DA],
                                    blocks[:].rearrange("p g h d -> p (g h d)"), ALU.mult).then_inc(delta_done.sem, 1)

                def attn_low(b):
                    wait(dve, attnT_hi, s, b)
                    v.scalar_tensor_tensor(AT[:, b, LO], TP[b][:], ATTN_UP, AT[:, b, HI],
                                           ALU.mult, ALU.subtract).then_inc(attnT_lo.sem, 1)

                def add_out(b):
                    wait(dve, out_filled, s, b)
                    if b == 0:
                        wait(dve, x1bo_done, s)
                        if FINISH:
                            wait(dve, y_done, back, 1)
                            wait(dve, var2_done, back)
                    v.scalar_tensor_tensor(X2[:, b], PJ[b][:], out_scale[:], X1BO[:, st.parity(0), b],
                                           ALU.mult, ALU.add).then_inc(x2_done.sem, 1)
                    wait(dve, x2_done, s, b)
                    stats(X2[:, b], raw2, stat2, stat2_raw, stat2_done, s, b)

                def back_gain(b, i, last=False):
                    if FRONT:
                        wait(dve, x1_done, f, b)
                    elif PROJECT:
                        wait(dve, x1_done, n, b)
                    elif last:
                        wait(dve, y_done, back, b)
                    wait(dve, stat2_done, i, b)
                    v.scalar_tensor_tensor(GAINED[:, b], X2[:, b], stat2[:, b, 0:1], gain[:],
                                           ALU.subtract, ALU.mult).then_inc(x2_gained.sem, 1)

                def back_y(b, i, last=False):
                    wait(dve, x2_gained, i, b)
                    if last:
                        dve.wait_ge(last_rstd, b + 1)
                        dve.wait_ge(last_shifted, b + 1)
                        wait(dve, y_stored, back)
                    elif b == 0:
                        wait(dve, rstd2_done, i)
                        wait(dve, x2b_done, i)
                        if st.has(-2):
                            wait(dve, y_stored, st.chunk(-2))
                    v.scalar_tensor_tensor(Y[:, b], GAINED[:, b], rstd2[:, b:b + 1], X2[:, b],
                                           ALU.mult, ALU.add).then_inc(y_done.sem, 1)

                if FRONT:
                    front_stats(0)
                    front_stats(1)
                    front_gain(0)
                    front_gain(1)
                if FRONT and not PROJECT:
                    front_x1(0)
                    front_stats1(0)
                    front_x1(1)
                    row_sums(0)
                    front_stats1(1)
                    scales(0)
                    w_low(0)
                    x_low(0)
                    x_low(1)
                    row_sums(1)
                    w_low(1)
                    scales(1)
                    return
                if ATTEND and not PROJECT:
                    back_gain(0, back)
                    back_gain(1, back)
                    mask(0, 0)
                    mask(0, 2)
                    split_a(0, 0)
                    mask(1, 0)
                    split_a(0, 2)
                    mask(1, 2)
                    quotient(0, 0)
                    split_a(1, 0)
                    quotient(0, 1)
                    split_a(1, 2)
                    quotient(1, 0)
                    quotient(1, 1)
                    attn_low(0)
                    back_y(0, back)
                    back_y(1, back)
                    attn_low(1)
                    add_out(0)
                    back_gain(0, s, True)
                    add_out(1)
                    back_gain(1, s, True)
                    back_y(0, s, True)
                    back_y(1, s, True)
                    return
                if PROJECT:
                    phi_k(0)
                if PROJECT and not FINISH:
                    phi_k(1)
                    low_k(0)
                    low_k(1)
                if PROJECT and not ATTEND:
                    w_low(2)
                if ATTEND:
                    mask(0, 0)
                if PROJECT and FINISH:
                    phi_k(1)
                if FRONT:
                    front_x1(0)
                    front_x1(1)
                if PROJECT and FINISH:
                    low_k(0)
                if ATTEND:
                    mask(0, 2)
                if FRONT:
                    front_stats1(0)
                if PROJECT and FINISH:
                    low_k(1)
                if PROJECT:
                    phi_q(0)
                if FRONT:
                    front_stats1(1)
                if PROJECT:
                    phi_q(1)
                    low_q(0)
                if ATTEND:
                    mask(1, 0)
                if FINISH:
                    back_gain(0, back)
                if ATTEND:
                    quotient(0, 0)
                if PROJECT:
                    low_q(1)
                if ATTEND:
                    mask(1, 2)
                if FINISH:
                    back_gain(1, back)
                if PROJECT:
                    low_v(0)
                if ATTEND:
                    quotient(0, 1)
                    delta(0, 0)
                if PROJECT:
                    low_v(1)
                if ATTEND:
                    quotient(1, 0)
                    delta(0, 1)
                    attn_low(0)
                    quotient(1, 1)
                    delta(1, 0)
                    delta(1, 1)
                    attn_low(1)
                if FRONT:
                    x_low(0)
                if FINISH:
                    back_y(0, back)
                    back_y(1, back)
                if ATTEND:
                    add_out(0)
                    add_out(1)
                if FRONT:
                    x_low(1)
                if PROJECT and not ATTEND:
                    w_low(3)

            run_first(body)
            run(dve, body)

        @block.tensor
        def _(pe):
            t_ = nc.tensor
            pe.wait_ge(consts_done, 1)
            pe.wait_ge(zeroed, 1)

            def w_transposes(first, last):
                for k in range(first, last):
                    m, c = W_ORDER[k // GROUPS], k % GROUPS
                    pe.wait_ge(w_loaded[m], 16)
                    if k >= W_REUSE:
                        pe.wait_ge(wT_lo, k - len(SC + AV) + 1)
                    for o in range(GROUPS):
                        ins = t_.transpose(W_BANKS[k][:, o * P:(o + 1) * P],
                                           wnat[m][:, o, c * P:(c + 1) * P], ident[:])
                    ins.then_inc(wT_filled, 1)

            def body(st):
                s, n, f, back = st.chunk(0), st.chunk(1), st.chunk(2), st.chunk(-1)
                PROJECT, ATTEND, FRONT, FINISH = st.has(1), st.has(0), st.has(2), st.has(-1)
                cur, nxt = st.parity(0), st.parity(1)

                def x_transposes(b):
                    wait(pe, xn_done, f, b)
                    if ATTEND:
                        wait(pe, attnT_lo, s, b)
                    elif PROJECT:
                        wait(pe, kT_copied, n, b)
                    for c in range(GROUPS):
                        ins = t_.transpose(TP[b][:, c * P:(c + 1) * P], XN[:, b, c * P:(c + 1) * P], ident[:])
                    ins.then_inc(xT_filled.sem, 1)

                def project_q(pr):
                    if not ATTEND:
                        pe.wait_ge(wT_lo, 2 * GROUPS)
                    wait(pe, k_relu, n, pr)
                    for g in range(2):
                        fb = 2 * pr + g
                        todo = [(c, w, m) for c in range(GROUPS) for w, m in PASSES]
                        for c, w, m in todo:
                            ins = t_.matmul(PJ[pr][:, g * TOK:(g + 1) * TOK], wT[0][:, w, c, fb * P:(fb + 1) * P],
                                            XT[:, m, c, :], start=(c, w, m) == todo[0], stop=(c, w, m) == todo[-1])
                    ins.then_inc(q_filled.sem, 1)

                def project_k(b):
                    if not ATTEND:
                        pe.wait_ge(wT_lo, GROUPS)
                    wait(pe, xT_lo, n, b)
                    if FINISH:
                        wait(pe, x2_done, back, b)
                    elif ATTEND:
                        wait(pe, v_lo, s, b)
                    project(1, b, k_filled)

                def project_v(b):
                    if not ATTEND:
                        pe.wait_ge(wT_lo, 3 * GROUPS)
                    wait(pe, q_relu, n, b)
                    project(2, b, v_filled)

                def project(m_, b, filled):
                    todo = [(c, w, m) for c in range(GROUPS) for w, m in PASSES]
                    for c, w, m in todo:
                        ins = t_.matmul(PJ[b][:], XT[:, w, c, b * C:(b + 1) * C], wT[m_][:, m, c, :],
                                        start=(c, w, m) == todo[0], stop=(c, w, m) == todo[-1])
                    ins.then_inc(filled.sem, 1)

                def k_transposes(b):
                    wait(pe, k_lo, n, b)
                    wait(pe, xT_lo, n, b)
                    for half in (HI, LO):
                        for c in range(GROUPS):
                            at = (half * GROUPS + c) * P
                            ins = t_.transpose(TP16[b][:, at:at + P], KN[nxt][:, b, half, c * P:(c + 1) * P], ident16[:])
                    ins.then_inc(kT_filled.sem, 1)

                def scores(b, hg):
                    k = b * GROUPS + hg
                    if k == 0:
                        pair_wait(pe, q_stacked, st, 0, 16 * RESTACKS)
                        pair_wait(pe, k_stacked, st, 0, 16 * RESTACKS)
                    reader = sc_copied if hg % 2 else sc_masked
                    if k >= 2:
                        wait(pe, reader, s, k // 2 - 1)
                    elif FINISH:
                        wait(pe, reader, back, 3)
                    for h in range(QUADS):
                        head = hg * QUADS + h
                        ins = t_.matmul(SC[hg % 2][:, h * C:(h + 1) * C], KS[cur][0:STACK, head, b * C:(b + 1) * C],
                                        QS[cur][0:STACK, head, b * C:(b + 1) * C], start=True, stop=True)
                    ins.then_inc(sc_filled.sem, 1)

                def attend(b, hf):
                    wait(pe, a_lo, s, b * GROUPS + 2 * hf + 1)
                    if not PROJECT:
                        pe.wait_ge(a_lo_even, 2 * b + hf + 1)
                    if FINISH and hf == 0:
                        wait(pe, s_lo, back, b)
                    if b == 1:
                        wait(pe, attn_done, s, hf)
                    elif FINISH:
                        wait(pe, attn_done, back, 2 + hf)
                    for g in range(2):
                        hg = 2 * hf + g
                        w_ = QUADS * DA
                        for w, m in PASSES:
                            t_.matmul(AV[hf][:, g * w_:(g + 1) * w_], QT[cur][:, w, hg, b * C:(b + 1) * C],
                                      SH[:, b, m, hf, g * w_:(g + 1) * w_], start=(w, m) == PASSES[0], stop=False)
                        for h in range(QUADS):
                            for w, m in PASSES:
                                ins = t_.matmul(AV[hf][:, g * w_ + h * DA:g * w_ + (h + 1) * DA],
                                                A[:, b, w, hg, h * C:(h + 1) * C], VN[cur][:, b, m, hg * QUADS + h, :],
                                                start=False, stop=(h == QUADS - 1 and (w, m) == PASSES[-1]))
                    ins.then_inc(av_filled.sem, 1)

                def update(b, hf):
                    w_ = QUADS * DA
                    if b == 1:
                        wait(pe, delta_done, s, hf)
                    else:
                        wait(pe, v_lo, n, hf)
                    for g in range(2):
                        hg = 2 * hf + g
                        for w, m in PASSES:
                            ins = t_.matmul(PJ[hf][:, g * w_:(g + 1) * w_], KN[cur][:, b, w, hg * P:(hg + 1) * P],
                                            VN[cur][:, b, m, hg * QUADS:(hg + 1) * QUADS, :],
                                            start=(w, m) == PASSES[0], stop=(w, m) == PASSES[-1])
                    ins.then_inc(st_filled.sem, 1)

                def attn_transposes(b):
                    wait(pe, attn_done, s, 2 * b + 1)
                    if PROJECT:
                        wait(pe, kT_copied, n, b)
                    else:
                        wait(pe, attnT_lo, back, b)
                    for c in range(GROUPS):
                        ins = t_.transpose(TP[b][:, c * P:(c + 1) * P], ATTN[:, b, c * P:(c + 1) * P], ident[:])
                    ins.then_inc(attnT_filled.sem, 1)

                def project_out(b):
                    wait(pe, attnT_lo, s, b)
                    if PROJECT:
                        wait(pe, delta_done, s, 2 + b)
                    else:
                        wait(pe, x2_done, back, b)
                    todo = [(c, w, m) for c in range(GROUPS) for w, m in PASSES]
                    for c, w, m in todo:
                        ins = t_.matmul(PJ[b][:], AT[:, b, w, c * C:(c + 1) * C], wT[3][:, m, c, :],
                                        start=(c, w, m) == todo[0], stop=(c, w, m) == todo[-1])
                    ins.then_inc(out_filled.sem, 1)

                if FRONT and not PROJECT:
                    w_transposes(0, W_REUSE)
                    x_transposes(0)
                    x_transposes(1)
                    w_transposes(W_REUSE, 2 * GROUPS)
                    return
                if ATTEND and not PROJECT:
                    scores(0, 0)
                    scores(0, 1)
                    scores(0, 2)
                    scores(0, 3)
                    scores(1, 0)
                    scores(1, 1)
                    attend(0, 0)
                    scores(1, 2)
                    scores(1, 3)
                    attend(0, 1)
                    attend(1, 0)
                    attend(1, 1)
                    attn_transposes(0)
                    attn_transposes(1)
                    project_out(0)
                    project_out(1)
                    return
                if PROJECT:
                    project_k(0)
                    project_k(1)
                if PROJECT and not ATTEND:
                    w_transposes(2 * GROUPS, 3 * GROUPS)
                if ATTEND and FINISH:
                    scores(0, 0)
                    scores(0, 1)
                if PROJECT:
                    project_q(0)
                if ATTEND and not FINISH:
                    project_q(1)
                    pe.wait_ge(wT_lo, 4 * GROUPS)
                    scores(0, 0)
                    scores(0, 1)
                if ATTEND:
                    scores(0, 2)
                    scores(0, 3)
                if PROJECT and (FINISH or not ATTEND):
                    project_q(1)
                if PROJECT:
                    k_transposes(0)
                    k_transposes(1)
                if PROJECT and not ATTEND:
                    w_transposes(3 * GROUPS, 4 * GROUPS)
                if ATTEND:
                    scores(1, 0)
                    attend(0, 0)
                    scores(1, 1)
                if PROJECT:
                    project_v(0)
                if ATTEND:
                    attend(0, 1)
                    scores(1, 2)
                    scores(1, 3)
                if PROJECT:
                    project_v(1)
                if ATTEND:
                    update(0, 0)
                    attend(1, 0)
                    attn_transposes(0)
                    update(0, 1)
                    attend(1, 1)
                    update(1, 0)
                if FRONT:
                    x_transposes(0)
                if ATTEND:
                    update(1, 1)
                    attn_transposes(1)
                    project_out(0)
                    project_out(1)
                if FRONT:
                    x_transposes(1)

            run_first(body)
            run(pe, body)


_INS = ['L0_attn_x', 'L0_attn_Wq', 'L0_attn_Wk', 'L0_attn_Wv', 'L0_attn_Wo', 'L0_attn_bo', 'L0_ffn_ln_g', 'L0_ffn_ln_b']
_OUTS = [((BATCH, LEN, E), 'float32')]


def kernel(**inputs):
    import numpy as _np
    import concourse.bacc as _bacc
    from concourse import mybir as _mybir
    from concourse.bass_utils import run_bass_kernel_spmd as _run

    nc = _bacc.Bacc("TRN2", target_bir_lowering=False, num_devices=1)
    arrays, args = {}, []
    for name in _INS:
        a = _np.ascontiguousarray(inputs[name])
        arrays[f"in_{name}_dram"] = a
        args.append(nc.dram_tensor(f"in_{name}_dram", a.shape, _mybir.dt.from_np(a.dtype), kind="ExternalInput").ap())
    for i, (shape, dtype) in enumerate(_OUTS):
        dt = _mybir.dt.from_np(_np.dtype(dtype))
        args.append(nc.dram_tensor(f"out_{i}_dram", shape, dt, kind="ExternalOutput").ap())
    build(nc, *args)
    r = _run(nc, [arrays], core_ids=[0])
    got = tuple(r.results[0][f"out_{i}_dram"] for i in range(len(_OUTS)))
    return got[0]
```
